# Optimizing a Trainium2 kernel written in Bass

```python
import numpy as np
import jax
import jax.numpy as jnp

def _softmax(x, axis=-1):
    return jax.nn.softmax(x, axis=axis)

def _gelu(x):
    return jax.nn.gelu(x, approximate=True)

def _silu(x):
    return jax.nn.silu(x)

def _sigmoid(x):
    return jax.nn.sigmoid(x)

def _layernorm(x, axis=-1, eps=1e-05):
    m = jnp.mean(x, axis=axis, keepdims=True)
    v = jnp.var(x, axis=axis, keepdims=True)
    return (x - m) / jnp.sqrt(v + eps)

def _scatter_add(tgt, idx, src, axis=0):
    return tgt.at[idx].add(src)

def _segment_sum(src, seg, n):
    return jax.ops.segment_sum(src, seg, n)
kernel_name = 'mk_hybrid_d1_jaxref_r8_b8727e'

def setup_inputs(seed: int=0):
    np.random.seed(seed)
    _w = jnp.asarray

    def _L0_attn_a_setup():
        import jax, jax.numpy as jnp
        import numpy as np
        N_HIDDEN = 256
        N_HEADS = 64
        EXPAND = 2
        D_STATE = 128
        D_CONV = 4
        CHUNK = 128
        DT_MIN = 0.001
        DT_MAX = 0.1
        INNER = EXPAND * N_HIDDEN
        HEAD_DIM = INNER // N_HEADS
        CONV_DIM = INNER + 2 * D_STATE
        D_IN_PROJ = 2 * INNER + 2 * D_STATE + N_HEADS
        EPS = 1e-06

        def _segsum(x):
            t = x.shape[-1]
            cs = jnp.cumsum(x, axis=-1)
            seg = cs[..., :, None] - cs[..., None, :]
            mask = jnp.tril(jnp.ones((t, t), dtype=bool))
            return jnp.where(mask, seg, -jnp.inf)

        def _ssd(x, dt, a, b_mat, c_mat, d, dt_bias):
            bsz, seq, h, p = x.shape
            dt = jnp.clip(jax.nn.softplus(dt + dt_bias), DT_MIN, DT_MAX)
            d_res = d.reshape(1, 1, h, 1) * x
            x_disc = x * dt[..., None]
            a_disc = a * dt
            ch = lambda t_: t_.reshape(bsz, seq // CHUNK, CHUNK, *t_.shape[2:])
            x_blk, b_blk, c_blk = (ch(x_disc), ch(b_mat), ch(c_mat))
            a_blk = jnp.transpose(ch(a_disc), (0, 3, 1, 2))
            a_cum = jnp.cumsum(a_blk, axis=-1)
            l_mat = jnp.exp(_segsum(a_blk))
            y_diag = jnp.einsum('bclhn,bcshn,bhcls,bcshp->bclhp', c_blk, b_blk, l_mat, x_blk)
            decay_states = jnp.exp(a_cum[..., -1:] - a_cum)
            states = jnp.einsum('bclhn,bhcl,bclhp->bchpn', b_blk, decay_states, x_blk)
            states = jnp.concatenate([jnp.zeros_like(states[:, :1]), states], axis=1)
            a_end = jnp.pad(a_cum[..., -1], ((0, 0), (0, 0), (1, 0)))
            decay_chunk = jnp.exp(_segsum(a_end))
            new_states = jnp.einsum('bhzc,bchpn->bzhpn', decay_chunk, states)
            states = new_states[:, :-1]
            y_off = jnp.einsum('bclhn,bchpn,bhcl->bclhp', c_blk, states, jnp.exp(a_cum))
            y = (y_diag + y_off).reshape(bsz, seq, h, p)
            return y + d_res
        key = jax.random.key(seed)
        ks = jax.random.split(key, 10)
        B, L = (2, 256)
        s = lambda fan_in: 1.0 / np.sqrt(fan_in)
        return {'x': jax.random.normal(ks[0], (B, L, N_HIDDEN), jnp.float32), 'W_in': jax.random.normal(ks[1], (N_HIDDEN, D_IN_PROJ), jnp.float32) * s(N_HIDDEN), 'b_in': jnp.zeros((D_IN_PROJ,), jnp.float32), 'conv_w': jax.random.normal(ks[2], (D_CONV, 1, CONV_DIM), jnp.float32) * s(D_CONV), 'conv_b': jnp.zeros((CONV_DIM,), jnp.float32), 'A_log': jnp.log(jnp.arange(1, N_HEADS + 1, dtype=jnp.float32)), 'dt_bias': jax.random.normal(ks[3], (N_HEADS,), jnp.float32) * 0.1, 'D_param': jnp.ones((N_HEADS,), jnp.float32), 'norm_w': jnp.ones((INNER,), jnp.float32), 'W_out': jax.random.normal(ks[4], (INNER, N_HIDDEN), jnp.float32) * s(INNER), 'b_out': jnp.zeros((N_HIDDEN,), jnp.float32)}
    _L0_attn_a_in = _L0_attn_a_setup()

    def _L0_attn_b_setup():
        import jax, jax.numpy as jnp
        import numpy as np
        HQ, HKV, HD = (32, 8, 64)
        G = HQ // HKV
        SCALE = HD ** (-0.5)

        def _rope(x, offset=0):
            B, L, H, hd = x.shape
            inv = 1.0 / 10000.0 ** (jnp.arange(0, hd, 2, dtype=jnp.float32) / hd)
            pos = jnp.arange(offset, offset + L, dtype=jnp.float32)
            f = pos[:, None] * inv[None, :]
            c = jnp.cos(f)[None, :, None, :]
            s = jnp.sin(f)[None, :, None, :]
            x1, x2 = (x[..., 0::2], x[..., 1::2])
            out = jnp.stack([x1 * c - x2 * s, x1 * s + x2 * c], axis=-1)
            return out.reshape(x.shape)
        key = jax.random.key(seed)
        ks = jax.random.split(key, 5)
        B, L, D = (2, 256, 256)
        w = 0.02
        return {'x': jax.random.normal(ks[0], (B, L, D), dtype=jnp.float32), 'Wq': jax.random.normal(ks[1], (HQ * HD, D), dtype=jnp.float32) * w, 'Wk': jax.random.normal(ks[2], (HKV * HD, D), dtype=jnp.float32) * w, 'Wv': jax.random.normal(ks[3], (HKV * HD, D), dtype=jnp.float32) * w, 'Wo': jax.random.normal(ks[4], (D, HQ * HD), dtype=jnp.float32) * w}
    _L0_attn_b_in = _L0_attn_b_setup()

    def _L0_ffn_setup():
        import jax, jax.numpy as jnp
        import numpy as np
        EPS = 1e-05
        ROPE_BASE = 150000.0
        NHEADS = 32
        KVHEADS = 8
        HEAD_DIM = 64
        TOP_K = 4

        def _rms(x, w):
            return x * jax.lax.rsqrt(jnp.mean(x * x, -1, keepdims=True) + EPS) * w

        def _rope(q, k):
            S, hd = (q.shape[1], q.shape[-1])
            half = hd // 2
            inv = 1.0 / ROPE_BASE ** (jnp.arange(half, dtype=jnp.float32) / half)
            ang = jnp.arange(S, dtype=jnp.float32)[:, None] * inv
            cos = jnp.concatenate([jnp.cos(ang), jnp.cos(ang)], -1)[None, :, None, :]
            sin = jnp.concatenate([jnp.sin(ang), jnp.sin(ang)], -1)[None, :, None, :]

            def rot(t):
                t1, t2 = (t[..., :half], t[..., half:])
                return jnp.concatenate([-t2, t1], -1)
            return (q * cos + rot(q) * sin, k * cos + rot(k) * sin)
        key = jax.random.key(seed)
        ks = jax.random.split(key, 12)
        B, S, D, H, E = (1, 128, 256, 256, 16)
        s = 0.02
        return {'x': jax.random.normal(ks[0], (B, S, D), jnp.float32), 'ln_w': jnp.ones((D,), jnp.float32), 'ff_ln_w': jnp.ones((D,), jnp.float32), 'wq': jax.random.normal(ks[1], (D, NHEADS * HEAD_DIM), jnp.float32) * s, 'wk': jax.random.normal(ks[2], (D, KVHEADS * HEAD_DIM), jnp.float32) * s, 'wv': jax.random.normal(ks[3], (D, KVHEADS * HEAD_DIM), jnp.float32) * s, 'wo': jax.random.normal(ks[4], (NHEADS * HEAD_DIM, D), jnp.float32) * s, 'wg': jax.random.normal(ks[5], (D, E), jnp.float32) * s, 'w1': jax.random.normal(ks[6], (E, D, H), jnp.float32) * s, 'w3': jax.random.normal(ks[7], (E, D, H), jnp.float32) * s, 'w2': jax.random.normal(ks[8], (E, H, D), jnp.float32) * s}
    _L0_ffn_in = _L0_ffn_setup()
    _d = {'L0_attn_a_x': _L0_attn_a_in['x'], 'L0_attn_a_W_in': _L0_attn_a_in['W_in'], 'L0_attn_a_b_in': _L0_attn_a_in['b_in'], 'L0_attn_a_conv_w': _L0_attn_a_in['conv_w'], 'L0_attn_a_conv_b': _L0_attn_a_in['conv_b'], 'L0_attn_a_A_log': _L0_attn_a_in['A_log'], 'L0_attn_a_dt_bias': _L0_attn_a_in['dt_bias'], 'L0_attn_a_D_param': _L0_attn_a_in['D_param'], 'L0_attn_a_norm_w': _L0_attn_a_in['norm_w'], 'L0_attn_a_W_out': _L0_attn_a_in['W_out'], 'L0_attn_a_b_out': _L0_attn_a_in['b_out'], 'L0_attn_b_Wq': _L0_attn_b_in['Wq'], 'L0_attn_b_Wk': _L0_attn_b_in['Wk'], 'L0_attn_b_Wv': _L0_attn_b_in['Wv'], 'L0_attn_b_Wo': _L0_attn_b_in['Wo'], 'L0_ffn_ln_w': _L0_ffn_in['ln_w'], 'L0_ffn_ff_ln_w': _L0_ffn_in['ff_ln_w'], 'L0_ffn_wq': _L0_ffn_in['wq'], 'L0_ffn_wk': _L0_ffn_in['wk'], 'L0_ffn_wv': _L0_ffn_in['wv'], 'L0_ffn_wo': _L0_ffn_in['wo'], 'L0_ffn_wg': _L0_ffn_in['wg'], 'L0_ffn_w1': _L0_ffn_in['w1'], 'L0_ffn_w3': _L0_ffn_in['w3'], 'L0_ffn_w2': _L0_ffn_in['w2']}
    _x0 = _d['L0_attn_a_x']
    _d['L0_attn_a_x'] = jax.random.normal(jax.random.fold_in(jax.random.key(seed), 1), (1, 1024, 256), dtype=_x0.dtype)
    del _x0
    return _d

def reference(L0_attn_a_x, L0_attn_a_W_in, L0_attn_a_b_in, L0_attn_a_conv_w, L0_attn_a_conv_b, L0_attn_a_A_log, L0_attn_a_dt_bias, L0_attn_a_D_param, L0_attn_a_norm_w, L0_attn_a_W_out, L0_attn_a_b_out, L0_attn_b_Wq, L0_attn_b_Wk, L0_attn_b_Wv, L0_attn_b_Wo, L0_ffn_ln_w, L0_ffn_ff_ln_w, L0_ffn_wq, L0_ffn_wk, L0_ffn_wv, L0_ffn_wo, L0_ffn_wg, L0_ffn_w1, L0_ffn_w3, L0_ffn_w2):

    def _L0_attn_a_ref(x, W_in, b_in, conv_w, conv_b, A_log, dt_bias, D_param, norm_w, W_out, b_out):
        import jax, jax.numpy as jnp
        import numpy as np
        N_HIDDEN = 256
        N_HEADS = 64
        EXPAND = 2
        D_STATE = 128
        D_CONV = 4
        CHUNK = 128
        DT_MIN = 0.001
        DT_MAX = 0.1
        INNER = EXPAND * N_HIDDEN
        HEAD_DIM = INNER // N_HEADS
        CONV_DIM = INNER + 2 * D_STATE
        D_IN_PROJ = 2 * INNER + 2 * D_STATE + N_HEADS
        EPS = 1e-06

        def _segsum(x):
            t = x.shape[-1]
            cs = jnp.cumsum(x, axis=-1)
            seg = cs[..., :, None] - cs[..., None, :]
            mask = jnp.tril(jnp.ones((t, t), dtype=bool))
            return jnp.where(mask, seg, -jnp.inf)

        def _ssd(x, dt, a, b_mat, c_mat, d, dt_bias):
            bsz, seq, h, p = x.shape
            dt = jnp.clip(jax.nn.softplus(dt + dt_bias), DT_MIN, DT_MAX)
            d_res = d.reshape(1, 1, h, 1) * x
            x_disc = x * dt[..., None]
            a_disc = a * dt
            ch = lambda t_: t_.reshape(bsz, seq // CHUNK, CHUNK, *t_.shape[2:])
            x_blk, b_blk, c_blk = (ch(x_disc), ch(b_mat), ch(c_mat))
            a_blk = jnp.transpose(ch(a_disc), (0, 3, 1, 2))
            a_cum = jnp.cumsum(a_blk, axis=-1)
            l_mat = jnp.exp(_segsum(a_blk))
            y_diag = jnp.einsum('bclhn,bcshn,bhcls,bcshp->bclhp', c_blk, b_blk, l_mat, x_blk)
            decay_states = jnp.exp(a_cum[..., -1:] - a_cum)
            states = jnp.einsum('bclhn,bhcl,bclhp->bchpn', b_blk, decay_states, x_blk)
            states = jnp.concatenate([jnp.zeros_like(states[:, :1]), states], axis=1)
            a_end = jnp.pad(a_cum[..., -1], ((0, 0), (0, 0), (1, 0)))
            decay_chunk = jnp.exp(_segsum(a_end))
            new_states = jnp.einsum('bhzc,bchpn->bzhpn', decay_chunk, states)
            states = new_states[:, :-1]
            y_off = jnp.einsum('bclhn,bchpn,bhcl->bclhp', c_blk, states, jnp.exp(a_cum))
            y = (y_diag + y_off).reshape(bsz, seq, h, p)
            return y + d_res
        B, L, _ = x.shape
        zxbcdt = x @ W_in + b_in
        z = zxbcdt[..., :INNER]
        xBC = zxbcdt[..., INNER:INNER + CONV_DIM]
        dt = zxbcdt[..., -N_HEADS:]
        xp = jnp.pad(xBC, ((0, 0), (D_CONV - 1, 0), (0, 0)))
        xBC = jax.lax.conv_general_dilated(xp, conv_w, window_strides=(1,), padding='VALID', dimension_numbers=('NWC', 'WIO', 'NWC'), feature_group_count=CONV_DIM) + conv_b
        xBC = jax.nn.silu(xBC)
        x_ssm = xBC[..., :INNER].reshape(B, L, N_HEADS, HEAD_DIM)
        b_mat = jnp.broadcast_to(xBC[..., INNER:INNER + D_STATE][:, :, None, :], (B, L, N_HEADS, D_STATE))
        c_mat = jnp.broadcast_to(xBC[..., INNER + D_STATE:][:, :, None, :], (B, L, N_HEADS, D_STATE))
        a = -jnp.exp(A_log)
        y = _ssd(x_ssm, dt, a, b_mat, c_mat, D_param, dt_bias)
        y = y.reshape(B, L, INNER)
        y = y * jax.nn.silu(z)
        y = y * jax.lax.rsqrt(jnp.mean(y * y, axis=-1, keepdims=True) + EPS) * norm_w
        return y @ W_out + b_out

    def _L0_attn_b_ref(x, Wq, Wk, Wv, Wo):
        import jax, jax.numpy as jnp
        import numpy as np
        HQ, HKV, HD = (32, 8, 64)
        G = HQ // HKV
        SCALE = HD ** (-0.5)

        def _rope(x, offset=0):
            B, L, H, hd = x.shape
            inv = 1.0 / 10000.0 ** (jnp.arange(0, hd, 2, dtype=jnp.float32) / hd)
            pos = jnp.arange(offset, offset + L, dtype=jnp.float32)
            f = pos[:, None] * inv[None, :]
            c = jnp.cos(f)[None, :, None, :]
            s = jnp.sin(f)[None, :, None, :]
            x1, x2 = (x[..., 0::2], x[..., 1::2])
            out = jnp.stack([x1 * c - x2 * s, x1 * s + x2 * c], axis=-1)
            return out.reshape(x.shape)
        B, L, D = x.shape
        q = (x @ Wq.T).reshape(B, L, HQ, HD)
        k = (x @ Wk.T).reshape(B, L, HKV, HD)
        v = (x @ Wv.T).reshape(B, L, HKV, HD)
        q = _rope(q)
        k = _rope(k)
        qh = q.transpose(0, 2, 1, 3).reshape(B, HKV, G, L, HD)
        kh = k.transpose(0, 2, 1, 3)
        vh = v.transpose(0, 2, 1, 3)
        attn = jnp.einsum('bkgqd,bkld->bkgql', qh, kh) * SCALE
        causal = jnp.arange(L)[:, None] >= jnp.arange(L)[None, :]
        attn = jnp.where(causal[None, None, None], attn, -jnp.inf)
        p = jax.nn.softmax(attn, axis=-1)
        out = jnp.einsum('bkgql,bkld->bkgqd', p, vh)
        out = out.reshape(B, HQ, L, HD).transpose(0, 2, 1, 3).reshape(B, L, HQ * HD)
        return out @ Wo.T

    def _L0_ffn_ref(x, ln_w, ff_ln_w, wq, wk, wv, wo, wg, w1, w3, w2):
        import jax, jax.numpy as jnp
        import numpy as np
        EPS = 1e-05
        ROPE_BASE = 150000.0
        NHEADS = 32
        KVHEADS = 8
        HEAD_DIM = 64
        TOP_K = 4

        def _rms(x, w):
            return x * jax.lax.rsqrt(jnp.mean(x * x, -1, keepdims=True) + EPS) * w

        def _rope(q, k):
            S, hd = (q.shape[1], q.shape[-1])
            half = hd // 2
            inv = 1.0 / ROPE_BASE ** (jnp.arange(half, dtype=jnp.float32) / half)
            ang = jnp.arange(S, dtype=jnp.float32)[:, None] * inv
            cos = jnp.concatenate([jnp.cos(ang), jnp.cos(ang)], -1)[None, :, None, :]
            sin = jnp.concatenate([jnp.sin(ang), jnp.sin(ang)], -1)[None, :, None, :]

            def rot(t):
                t1, t2 = (t[..., :half], t[..., half:])
                return jnp.concatenate([-t2, t1], -1)
            return (q * cos + rot(q) * sin, k * cos + rot(k) * sin)
        B, S, D = x.shape
        h = _rms(x, ln_w)
        q = (h @ wq).reshape(B, S, NHEADS, HEAD_DIM)
        k = (h @ wk).reshape(B, S, KVHEADS, HEAD_DIM)
        v = (h @ wv).reshape(B, S, KVHEADS, HEAD_DIM)
        q, k = _rope(q, k)
        g = NHEADS // KVHEADS
        k = jnp.repeat(k, g, axis=2)
        v = jnp.repeat(v, g, axis=2)
        scores = jnp.einsum('bqhd,bkhd->bhqk', q, k) / np.float32(np.sqrt(HEAD_DIM))
        causal = jnp.tril(jnp.ones((S, S), bool))
        scores = jnp.where(causal[None, None], scores, jnp.float32(-1e+30))
        attn = jax.nn.softmax(scores, -1)
        o = jnp.einsum('bhqk,bkhd->bqhd', attn, v).reshape(B, S, NHEADS * HEAD_DIM)
        x = x + o @ wo
        h = _rms(x, ff_ln_w)
        logits = h @ wg
        topv, topi = jax.lax.top_k(logits, TOP_K)
        gate = jax.nn.softmax(topv, -1)
        bidx = jnp.arange(B)[:, None, None]
        sidx = jnp.arange(S)[None, :, None]
        weights = jnp.zeros_like(logits).at[bidx, sidx, topi].set(gate)
        a = jax.nn.silu(jnp.einsum('bsd,edh->bseh', h, w1)) * jnp.einsum('bsd,edh->bseh', h, w3)
        y = jnp.einsum('bseh,ehd->bsed', a, w2)
        moe = jnp.einsum('bsed,bse->bsd', y, weights)
        return x + moe
    x = L0_attn_a_x
    x = x + _L0_attn_a_ref(_layernorm(x, axis=-1), L0_attn_a_W_in, L0_attn_a_b_in, L0_attn_a_conv_w, L0_attn_a_conv_b, L0_attn_a_A_log, L0_attn_a_dt_bias, L0_attn_a_D_param, L0_attn_a_norm_w, L0_attn_a_W_out, L0_attn_a_b_out)
    x = x + _L0_ffn_ref(_layernorm(x, axis=-1), L0_ffn_ln_w, L0_ffn_ff_ln_w, L0_ffn_wq, L0_ffn_wk, L0_ffn_wv, L0_ffn_wo, L0_ffn_wg, L0_ffn_w1, L0_ffn_w3, L0_ffn_w2)
    x = x + _L0_attn_b_ref(_layernorm(x, axis=-1), L0_attn_b_Wq, L0_attn_b_Wk, L0_attn_b_Wv, L0_attn_b_Wo)
    x = x + _L0_ffn_ref(_layernorm(x, axis=-1), L0_ffn_ln_w, L0_ffn_ff_ln_w, L0_ffn_wq, L0_ffn_wk, L0_ffn_wv, L0_ffn_wo, L0_ffn_wg, L0_ffn_w1, L0_ffn_w3, L0_ffn_w2)
    return x

_drawn_inputs = setup_inputs


def setup_inputs(seed=0):
    import zlib

    import numpy as np

    out = dict(_drawn_inputs(seed))
    spreads = {'L0_attn_a_b_in': (0.0, 0.1),
     'L0_attn_a_conv_b': (0.0, 0.1),
     'L0_attn_a_D_param': (1.0, 0.2),
     'L0_attn_a_norm_w': (1.0, 0.2),
     'L0_attn_a_b_out': (0.0, 0.1),
     'L0_ffn_ln_w': (1.0, 0.6),
     'L0_ffn_ff_ln_w': (1.0, 0.6)}
    factors = {'L0_attn_a_dt_bias': 8.0,
     'L0_attn_b_Wq': 8.0,
     'L0_attn_b_Wk': 8.0,
     'L0_attn_b_Wv': 3.027,
     'L0_attn_b_Wo': 3.052,
     'L0_ffn_wq': 8.0,
     'L0_ffn_wk': 8.0,
     'L0_ffn_wg': 8.0,
     'L0_ffn_w1': 8.0,
     'L0_ffn_w3': 8.0,
     'L0_ffn_w2': 8.0}
    for name, (base, spread) in spreads.items():
        noise = np.random.default_rng([zlib.crc32(name.encode()), seed]).standard_normal(out[name].shape)
        drawn = base * np.exp(spread * noise) if base else spread * noise
        out[name] = jnp.asarray(drawn.astype(out[name].dtype))
    for name, factor in factors.items():
        out[name] = (out[name] * factor).astype(out[name].dtype)
    return out
```

```python
from contextlib import ExitStack

import numpy as np
import concourse.bass as bass
from concourse import mybir

F32 = mybir.dt.float32
F32R = mybir.dt.float32r
BF16 = mybir.dt.bfloat16
U32 = mybir.dt.uint32
ALU = mybir.AluOpType
ACT = mybir.ActivationFunctionType
AX = mybir.AxisListType

P = 128
L = 1024
D = 256
NT = L // P
DK = D // P
HQ, HKV, HD = 32, 8, 64
G = HQ // HKV
GW = (G + 2) * HD
STEPS = HKV * NT
BODY = 2 * NT
NE, TOPK, HH = 16, 4, 256
INNER, DST, NH, HP, TAPS = 512, 128, 64, 8, 4
CH = 64
CONVD = INNER + 2 * DST
NX = CONVD // P
NZ = INNER // P
NEG = -1.0e30


def ax(ap, n):
    return ap.unsqueeze(1).broadcast_to([ap.shape[0], n, ap.shape[1]])


def bx(ap, n):
    return ap.unsqueeze(len(ap.shape)).broadcast_to(list(ap.shape) + [n])


class Core:

    def __init__(self, nc, ctx, dram):
        self.nc, self.ctx, self.dram = nc, ctx, dram
        self.sems, self.before = {}, {}
        self.phase = 0
        sb = self.sb
        self.x = sb("x_res", [P, NT, D])
        self.u = sb("u_res", [P, NT, D])
        self.ident = sb("ident", [P, P])
        self.ident16 = sb("ident16", [P, P], BF16)
        self.causal16 = sb("causal16", [P, P], BF16)
        self.consts = sb("consts", [P, 256])
        self.ln_cols = sb("ln_cols", [P, 2, DK])
        self.psum = ctx.enter_context(nc.psum_tensor("banks", [P, 8, 512], F32))

    def sb(self, name, shape, dt=F32, ctx=None):
        return (ctx or self.ctx).enter_context(self.nc.sbuf_tensor(name, shape, dt))

    def sem(self, name):
        if name not in self.sems:
            self.sems[name] = self.ctx.enter_context(self.nc.semaphore(name))
            self.before[self.sems[name]] = 0
        return self.sems[name]

    def count(self, sem, n, loop=None):
        if loop is None:
            assert n >= 1
            return self.before[sem] + n
        return loop[0] * loop[1] + (self.before[sem] + n)

    def own(self, sem):
        self.before[sem] += 1
        return self.before[sem]

    def done(self, counts):
        for sem, n in counts.items():
            self.before[sem] += n



def normalise(c, src, layer, rms_eps, w_cols, hT, dst, splits=None, exact=True):
    nc, count, own = c.nc, c.count, c.own
    with ExitStack() as ctx:
        n = c.phase
        c.phase += 1
        cen = c.sb(f"nrm_cen{n}", [P, NT, D], ctx=ctx) if layer else src
        sq = c.sb(f"nrm_sq{n}", [P, NT, D], ctx=ctx)
        st = c.sb(f"nrm_st{n}", [P, 8, NT], ctx=ctx)
        mean, ssq, var, rstd, t0, r2 = (st[:, i, :] for i in range(6))
        hn = c.sb(f"nrm_h{n}", [P, NT, D], ctx=ctx) if rms_eps is not None else dst
        centred, squared, vard, rstdd, t0d, r2d = (
            c.sem(x) for x in ("nrm_centred", "nrm_squared", "nrm_var", "nrm_rstd", "nrm_t0", "nrm_r2"))
        normed, turned, evac, evac32 = (c.sem(x) for x in ("nrm_out", "nrm_turned", "nrm_evac", "nrm_evac32"))
        dve, pool = c.sem("dve_own"), c.sem("pool_own")
        banks = c.psum
        fused = layer and rms_eps is not None
        last_r = r2d if fused else rstdd

        with nc.Block() as block:
            @block.vector
            def _(v):
                if layer:
                    v.tensor_reduce(mean, src[:, :, :], AX.X, ALU.add).then_inc(dve, 1)
                    v.wait_ge(dve, own(dve))
                    v.tensor_scalar(mean, mean, 1.0 / D, None, ALU.mult).then_inc(dve, 1)
                    v.wait_ge(dve, own(dve))
                    v.tensor_tensor(cen[:, :, :], src[:, :, :], bx(mean, D), ALU.subtract).then_inc(centred, 1)
                v.wait_ge(squared, count(squared, 1))
                v.tensor_reduce(ssq, sq[:, :, :], AX.X, ALU.add).then_inc(dve, 1)
                v.wait_ge(dve, own(dve))
                eps = 1e-5 if layer else rms_eps
                v.tensor_scalar(var, ssq, 1.0 / D, None, ALU.mult).then_inc(dve, 1)
                v.wait_ge(dve, own(dve))
                v.tensor_scalar(t0, var, eps, None, ALU.add).then_inc(vard, 1)
                v.wait_ge(rstdd, count(rstdd, 1))
                if fused:
                    v.tensor_tensor(var, var, rstd, ALU.mult).then_inc(dve, 1)
                    v.wait_ge(dve, own(dve))
                    v.tensor_tensor(var, var, rstd, ALU.mult).then_inc(dve, 1)
                    v.wait_ge(dve, own(dve))
                    v.tensor_scalar(t0, var, rms_eps, None, ALU.add).then_inc(t0d, 1)
                    v.wait_ge(r2d, count(r2d, 1))
                    v.tensor_tensor(r2, r2, rstd, ALU.mult).then_inc(dve, 1)
                    v.wait_ge(dve, own(dve))
                for k in range(DK):
                    v.tensor_tensor(hn[:, :, k * P:(k + 1) * P], cen[:, :, k * P:(k + 1) * P],
                                    bx(r2 if fused else rstd, P), ALU.mult).then_inc(normed, 1)
                if fused:
                    v.tensor_tensor(dst[:, :, :], cen[:, :, :], bx(rstd, D), ALU.mult)
                if splits:
                    hi, lo = splits
                    for b in range(2 * DK):
                        k, half = b // 2, b % 2
                        cols = slice(half * 512, half * 512 + 512)
                        v.wait_ge(evac, count(evac, b + 1))
                        v.tensor_tensor(lo[:, k, cols], hT[:, k, cols], hi[:, k, cols].bitcast(F32),
                                        ALU.subtract)

            @block.gpsimd
            def _(g):
                g.memset(st[:, 7, :], -0.5).then_inc(pool, 1)
                g.wait_ge(pool, own(pool))
                g.wait_ge(vard, count(vard, 1))
                g.tensor_tensor(rstd, t0, st[:, 7, :], ALU.pow).then_inc(rstdd, 1)
                if fused:
                    g.wait_ge(t0d, count(t0d, 1))
                    g.tensor_tensor(r2, t0, st[:, 7, :], ALU.pow).then_inc(r2d, 1)

            @block.scalar
            def _(a):
                if layer:
                    a.wait_ge(centred, count(centred, 1))
                a.activation(sq[:, :, :], cen[:, :, :], ACT.Square).then_inc(squared, 1)
                for b in range(2 * DK):
                    k, half = b // 2, b % 2
                    cols = slice(half * 512, half * 512 + 512)
                    a.wait_ge(turned, count(turned, b + 1))
                    if w_cols is None:
                        ins = a.activation(hT[:, k, cols], banks[:, b, :], ACT.Copy)
                    else:
                        ins = a.activation(hT[:, k, cols], banks[:, b, :], ACT.Copy, scale=w_cols[:, k:k + 1])
                    if splits:
                        ins.then_inc(evac32, 1)
                        a.wait_ge(evac32, count(evac32, b + 1))
                        ins = a.activation(splits[0][:, k, cols], hT[:, k, cols], ACT.Copy)
                    ins.then_inc(evac, 1)

            @block.tensor
            def _(t):
                for b in range(2 * DK):
                    k, half = b // 2, b % 2
                    t.wait_ge(normed, count(normed, k + 1))
                    for j in range(4):
                        ins = t.transpose(banks[:, b, j * P:(j + 1) * P],
                                          hn[:, half * 4 + j, k * P:(k + 1) * P], c.ident[:, :])
                    ins.then_inc(turned, 1)
        c.done({centred: int(layer), squared: 1, vard: 1, rstdd: 1, t0d: int(fused), r2d: int(fused),
                normed: DK, turned: 2 * DK, evac: 2 * DK, evac32: 2 * DK if splits else 0})



def attention(c, hT, wqkv, wo, rope, acc):
    nc, count, own = c.nc, c.count, c.own
    banks = c.psum
    s_of = lambda h: banks[:, 2 * (h % 2):2 * (h % 2) + 2, :].rearrange("p b n -> p (b n)")
    pt = [banks[:, 4, :], banks[:, 5, :]]
    shared, o_ps = banks[:, 6, :], banks[:, 7, 0:G * HD]
    names = ["at_proj", "at_rope", "at_vcopy", "at_split", "at_qt", "at_qtev", "at_kt", "at_ktev", "at_ot",
             "at_otev", "at_s", "at_max", "at_exp", "at_t0", "at_t1", "at_ev0", "at_ev1", "at_pv", "at_norm",
             "at_op", "at_add", "at_rec", "at_sum", "at_hi"]
    (proj_done, rope_done, v_copied, split_done, qt_done, qt_evac, kt_done, kt_evac, ot_done, ot_evac, s_done,
     max_done, exp_done, t0_done, t1_done, ev0_done, ev1_done, pv_done, norm_done, op_done, add_done,
     rec_done, sum_done, hi_done) = (c.sem(x) for x in names)
    per_step = {s: 1 for s in (proj_done, rope_done, v_copied, split_done, qt_done, qt_evac, kt_done, kt_evac,
                               ot_done, ot_evac, norm_done, op_done, add_done, rec_done, sum_done)}
    per_step.update({s: 4 for s in (s_done, max_done, exp_done, t0_done, ev0_done, pv_done)})
    per_step[hi_done] = 2
    wqkv_f = wqkv[:, :, :].rearrange("p k n -> p (k n)")
    wo_f = wo[:, :, :].rearrange("p k n -> p (k n)")

    with ExitStack() as ctx:
        ph = c.phase
        c.phase += 1
        sb = lambda name, shape, dt=F32: c.sb(f"{name}{ph}", shape, dt, ctx)
        ra = sb("rope_a", [P, 5, HD])
        rb = sb("rope_b", [P, 5, HD])
        rs = sb("rope_sum", [P, 5, HD])
        qk = [sb(f"qk_parts{i}", [P, 6, P], F32R) for i in range(2)]
        qT = [sb(f"qT{i}", [P, G, P], F32R) for i in range(2)]
        kT = [sb(f"kT{i}", [P, 2, L], F32R) for i in range(2)]
        vv = [sb(f"v{i}", [P, NT, HD]) for i in range(2)]
        prob = [sb(f"prob{i}", [P, L]) for i in range(2)]
        pT = [sb(f"pT{i}", [P, L]) for i in range(2)]
        nmax = sb("nmax", [P, 4])
        sums = sb("sums", [P, 2, G])
        rec = sb("rec", [P, 2, G])
        o_tok = sb("o_tok", [P, G, HD])
        oT = sb("oT", [P, 2, P])

        def real(n, it):
            return it is not None or 0 <= n < STEPS

        def at(sem, n, j=1, it=None):
            k = per_step[sem]
            return count(sem, k * n + j, None if it is None else (it, k * BODY))

        def at_late(sem, n, h, it):
            k = 16 * (n // NT) + 4 * (n % NT - 4) + h + 1
            return count(sem, k, None if it is None else (it, 32))

        def cols(base, step, width, it):
            return slice(base, base + width) if it is None else bass.ds(it * step + base, width)

        def spans(eng, program):
            loops = STEPS // BODY - 1
            for n in range(-2, 2):
                program(n, None)
            with eng.Fori(0, loops, 1) as it:
                for n in range(2, 2 + BODY):
                    program(n, it)
            for n in range(2 + BODY * loops, STEPS + 1):
                program(n, None)

        def two_back(n, h):
            return (n, h - 2) if h >= 2 else (n - 1, h + 2)

        with nc.Block() as block:
            @block.tensor
            def _(pe):
                def step(n, it):
                    for h in range(G):
                        n2, h2 = two_back(n, h)
                        t2 = n2 % NT
                        i2 = (4 * n2 + h2) % 2
                        if real(n2, it):
                            pe.wait_ge(exp_done, at(exp_done, n2, h2 + 1, it))
                            for j in range(t2 + 1):
                                ins = pe.transpose(pt[j // 4][:, (j % 4) * P:(j % 4 + 1) * P],
                                                   prob[i2][:, j * P:(j + 1) * P], c.ident[:, :])
                                if j == min(t2, 3):
                                    ins.then_inc(t0_done, 1)
                            if t2 >= 4:
                                ins.then_inc(t1_done, 1)
                        if real(n, it):
                            t, par = n % NT, (n // NT) % 2
                            if h == 0:
                                pe.wait_ge(qt_evac, at(qt_evac, n, 1, it))
                                pe.wait_ge(kt_evac, at(kt_evac, n, 1, it))
                            s_ps, width = s_of(h), (t + 1) * P
                            for lo in range(0, width, 512):
                                hi = min(lo + 512, width)
                                for part in range(2):
                                    pe.matmul(s_ps[:, lo:hi], qT[n % 2][:, h, :], kT[par][:, part, lo:hi],
                                              start=part == 0, stop=part == 1 and hi < width)
                            pe.matmul(s_ps[:, width - P:width], c.ident16[:, :], c.causal16[:, :],
                                      start=False, stop=True).then_inc(s_done, 1)
                        if h == 0 and real(n + 2, it):
                            m = n + 2
                            t = m % NT
                            if real(n - 2, it):
                                pe.wait_ge(add_done, at(add_done, n - 2, 1, it))
                            elif real(n + 1, it):
                                pe.wait_ge(v_copied, at(v_copied, n + 1, 1, it))
                            for k in range(DK):
                                ins = pe.matmul(shared[:, 0:GW], hT[:, k, t * P:(t + 1) * P],
                                                wqkv_f[:, cols(k * HKV * GW + (m // NT) * GW, 2 * GW, GW, it)],
                                                start=k == 0, stop=k == DK - 1)
                            ins.then_inc(proj_done, 1)
                        if h == 1 and real(n + 1, it):
                            if real(n + 2, it):
                                pe.wait_ge(v_copied, at(v_copied, n + 2, 1, it))
                            elif real(n - 2, it):
                                pe.wait_ge(add_done, at(add_done, n - 2, 1, it))
                            pe.wait_ge(split_done, at(split_done, n + 1, 1, it))
                            for q in range(G):
                                ins = pe.transpose(shared[:, q * P:(q + 1) * P],
                                                   qk[(n + 1) % 2][:, q, :].bitcast(F32), c.ident[:, :])
                            ins.then_inc(qt_done, 1)
                        if h == 2:
                            if real(n + 1, it):
                                pe.wait_ge(qt_evac, at(qt_evac, n + 1, 1, it))
                                for q in range(2):
                                    ins = pe.transpose(shared[:, q * P:(q + 1) * P],
                                                       qk[(n + 1) % 2][:, 4 + q, :].bitcast(F32), c.ident[:, :])
                                ins.then_inc(kt_done, 1)
                            if real(n - 1, it):
                                if not real(n + 1, it) and real(n - 2, it):
                                    pe.wait_ge(add_done, at(add_done, n - 2, 1, it))
                                pe.wait_ge(norm_done, at(norm_done, n - 1, 1, it))
                                for j in range(2):
                                    ins = pe.transpose(shared[:, (2 + j) * P:(3 + j) * P],
                                                       o_tok[:, 2 * j:2 * j + 2, :].rearrange("p h d -> p (h d)"),
                                                       c.ident[:, :])
                                ins.then_inc(ot_done, 1)
                        if h == 3 and real(n - 1, it):
                            m = n - 1
                            if real(n + 1, it):
                                pe.wait_ge(kt_evac, at(kt_evac, n + 1, 1, it))
                            pe.wait_ge(ot_evac, at(ot_evac, m, 1, it))
                            for j in range(2):
                                ins = pe.matmul(shared[:, 0:D], oT[:, j, :],
                                                wo_f[:, cols((2 * (m // NT) + j) * D, 4 * D, D, it)],
                                                start=j == 0, stop=j == 1)
                            ins.then_inc(op_done, 1)
                        if real(n2, it):
                            pe.wait_ge(ev0_done, at(ev0_done, n2, h2 + 1, it))
                            if t2 >= 4:
                                pe.wait_ge(ev1_done, at_late(ev1_done, n2, h2, it))
                            if h2 == 0:
                                pe.wait_ge(v_copied, at(v_copied, n2, 1, it))
                                if real(n2 - 1, it):
                                    pe.wait_ge(norm_done, at(norm_done, n2 - 1, 1, it))
                            par = (n2 // NT) % 2
                            for j in range(t2 + 1):
                                ins = pe.matmul(o_ps[:, h2 * HD:(h2 + 1) * HD], pT[i2][:, j * P:(j + 1) * P],
                                                vv[par][:, j, :], start=j == 0, stop=j == t2)
                            ins.then_inc(pv_done, 1)
                spans(pe, step)

            @block.scalar
            def _(a):
                def step(n, it):
                    for h in range(G):
                        n2, h2 = two_back(n, h)
                        if real(n2, it):
                            a.wait_ge(t0_done, at(t0_done, n2, h2 + 1, it))
                            width = min(n2 % NT + 1, 4) * P
                            a.activation(pT[h2 % 2][:, 0:width], pt[0][:, 0:width], ACT.Copy).then_inc(ev0_done, 1)
                        n1, h1 = (n, h - 1) if h else (n - 1, 3)
                        if real(n1, it):
                            width = (n1 % NT + 1) * P
                            a.wait_ge(max_done, at(max_done, n1, h1 + 1, it))
                            a.activation(prob[h1 % 2][:, 0:width], s_of(h1)[:, 0:width], ACT.Exp,
                                         bias=nmax[:, h1:h1 + 1], scale=1.0,
                                         accum_out=sums[:, n1 % 2, h1:h1 + 1]).then_inc(exp_done, 1)
                        if h == 1 and real(n + 1, it):
                            a.wait_ge(qt_done, at(qt_done, n + 1, 1, it))
                            a.activation(qT[(n + 1) % 2][:, :, :].rearrange("p h n -> p (h n)"),
                                         shared, ACT.Copy, scale=float(HD) ** -0.5).then_inc(qt_evac, 1)
                        if h == 2 and real(n + 1, it):
                            m = n + 1
                            a.wait_ge(kt_done, at(kt_done, m, 1, it))
                            if real(n - 1, it):
                                a.wait_ge(ot_done, at(ot_done, n - 1, 1, it))
                            a.activation(kT[(m // NT) % 2][:, :, (m % NT) * P:(m % NT + 1) * P],
                                         shared[:, 0:2 * P].rearrange("p (a n) -> p a n", a=2), ACT.Copy).then_inc(kt_evac, 1)
                        if h == 2 and real(n - 1, it):
                            a.wait_ge(ot_done, at(ot_done, n - 1, 1, it))
                            a.activation(oT[:, :, :].rearrange("p a n -> p (a n)"),
                                         shared[:, 2 * P:4 * P], ACT.Copy).then_inc(ot_evac, 1)
                spans(a, step)

            @block.vector
            def _(v):
                def step(n, it):
                    for h in range(G):
                        n2, h2 = two_back(n, h)
                        if h == 2 and real(n - 1, it):
                            m = n - 1
                            v.wait_ge(exp_done, at(exp_done, m, 4, it))
                            v.reciprocal(rec[:, m % 2, :], sums[:, m % 2, :]).then_inc(rec_done, 1)
                            v.wait_ge(rec_done, at(rec_done, m, 1, it))
                            v.wait_ge(pv_done, at(pv_done, m, 4, it))
                            v.tensor_tensor(o_tok[:, :, :], o_ps.rearrange("p (h d) -> p h d", h=G),
                                            bx(rec[:, m % 2, :], HD), ALU.mult).then_inc(norm_done, 1)
                        if real(n2, it) and n2 % NT >= 4:
                            v.wait_ge(t1_done, at_late(t1_done, n2, h2, it))
                            width = (n2 % NT - 3) * P
                            v.tensor_copy(pT[h2 % 2][:, 512:512 + width], pt[1][:, 0:width]).then_inc(ev1_done, 1)
                        if real(n, it):
                            v.wait_ge(s_done, at(s_done, n, h + 1, it))
                            v.tensor_reduce(nmax[:, h:h + 1], s_of(h)[:, 0:(n % NT + 1) * P],
                                            AX.X, ALU.max, negate=True).then_inc(max_done, 1)
                        if h == 0 and real(n + 2, it):
                            m = n + 2
                            t = m % NT
                            v.wait_ge(proj_done, at(proj_done, m, 1, it))
                            if real(m - 1, it):
                                v.wait_ge(hi_done, at(hi_done, m - 1, 2, it))
                            qk_ps = shared[:, 0:5 * HD].rearrange("p (h d) -> p h d", h=5)
                            v.tensor_tensor(ra[:, :, :], qk_ps, ax(rope[:, 0, t, :], 5), ALU.mult)
                            v.tensor_tensor(rb[:, :, 0:HD // 2], qk_ps[:, :, HD // 2:HD],
                                            ax(rope[:, 1, t, 0:HD // 2], 5), ALU.mult)
                            v.tensor_tensor(rb[:, :, HD // 2:HD], qk_ps[:, :, 0:HD // 2],
                                            ax(rope[:, 1, t, HD // 2:HD], 5), ALU.mult).then_inc(rope_done, 1)
                            v.tensor_copy(vv[(m // NT) % 2][:, t, :], shared[:, GW - HD:GW]).then_inc(v_copied, 1)
                        if h == 3 and real(n - 1, it):
                            m = n - 1
                            v.wait_ge(op_done, at(op_done, m, 1, it))
                            v.tensor_tensor(acc[:, m % NT, :], acc[:, m % NT, :], shared[:, 0:D], ALU.add).then_inc(add_done, 1)
                spans(v, step)

            @block.gpsimd
            def _(g):
                def step(n, it):
                    if real(n + 2, it):
                        m = n + 2
                        parts = qk[m % 2]
                        g.wait_ge(rope_done, at(rope_done, m, 1, it))
                        if real(m - 2, it):
                            g.wait_ge(kt_done, at(kt_done, m - 2, 1, it))
                        if real(m - 1, it):
                            g.wait_ge(split_done, at(split_done, m - 1, 1, it))
                        g.tensor_tensor(rs[:, :, :], ra[:, :, :], rb[:, :, :], ALU.add).then_inc(sum_done, 1)
                        g.tensor_tensor(parts[:, 0:4, 0:HD], ra[:, 0:4, :], rb[:, 0:4, :], ALU.add).then_inc(hi_done, 1)
                        g.tensor_tensor(parts[:, 4, :].rearrange("p (a d) -> p a d", a=2),
                                        ax(ra[:, 4, :], 2), ax(rb[:, 4, :], 2), ALU.add).then_inc(hi_done, 1)
                        g.wait_ge(sum_done, at(sum_done, m, 1, it))
                        g.wait_ge(hi_done, at(hi_done, m, 2, it))
                        g.tensor_tensor(parts[:, 0:4, HD:P], rs[:, 0:4, :], parts[:, 0:4, 0:HD].bitcast(F32),
                                        ALU.subtract)
                        g.tensor_tensor(parts[:, 5, :].rearrange("p (a d) -> p a d", a=2),
                                        ax(rs[:, 4, :], 2),
                                        parts[:, 4, :].rearrange("p (a d) -> p a d", a=2).bitcast(F32),
                                        ALU.subtract).then_inc(split_done, 1)
                spans(g, step)

        counts = {s: k * STEPS for s, k in per_step.items()}
        counts.update({t1_done: 16 * HKV, ev1_done: 16 * HKV})
        c.done(counts)



def router(c, hT, wg, gates):
    nc, count, own = c.nc, c.count, c.own
    with ExitStack() as ctx:
        ph = c.phase
        c.phase += 1
        sb = lambda name, shape, dt=F32: c.sb(f"{name}{ph}", shape, dt, ctx)
        logits = sb("logits", [P, NT, NE])
        top = sb("top", [P, NT, 8])
        idx = sb("top_idx", [P, NT, 8], U32)
        idxf = sb("top_idxf", [P, NT, 8])
        ex = sb("top_exp", [P, NT, TOPK])
        den = sb("top_den", [P, NT])
        eq = sb("top_eq", [P, TOPK, NT, NE])
        wsum = sb("gate_rows", [P, NT, NE])
        logits_done, ready, exps = (c.sem(x) for x in ("rt_logits", "rt_shifted", "rt_exp"))
        dve = c.sem("dve_own")
        iota = c.consts[:, 0:NE]
        with nc.Block() as block:
            @block.tensor
            def _(pe):
                for t in range(NT):
                    for k in range(DK):
                        ins = pe.matmul(c.psum[:, 0, t * NE:(t + 1) * NE], hT[:, k, t * P:(t + 1) * P],
                                        wg[:, k, :], start=k == 0, stop=k == DK - 1)
                ins.then_inc(logits_done, 1)

            @block.scalar
            def _(a):
                a.wait_ge(ready, count(ready, 1))
                a.activation(ex[:, :, :], ex[:, :, :], ACT.Exp).then_inc(exps, 1)

            @block.vector
            def _(v):
                v.wait_ge(logits_done, count(logits_done, 1))
                v.tensor_copy(logits[:, :, :].rearrange("p t e -> p (t e)"), c.psum[:, 0, 0:NT * NE]).then_inc(dve, 1)
                v.wait_ge(dve, own(dve))
                for t in range(NT):
                    ins = v.max(top[:, t, :], logits[:, t, :])
                ins.then_inc(dve, 1)
                v.wait_ge(dve, own(dve))
                for t in range(NT):
                    ins = v.max_index(idx[:, t, :], top[:, t, :], logits[:, t, :])
                ins.then_inc(dve, 1)
                v.wait_ge(dve, own(dve))
                v.tensor_copy(idxf[:, :, :], idx[:, :, :])
                v.tensor_tensor(ex[:, :, :], top[:, :, 0:TOPK], bx(top[:, :, 0], TOPK), ALU.subtract).then_inc(ready, 1)
                v.wait_ge(exps, count(exps, 1))
                v.tensor_reduce(den[:, :], ex[:, :, :], AX.X, ALU.add).then_inc(dve, 1)
                v.wait_ge(dve, own(dve))
                v.reciprocal(den[:, :], den[:, :]).then_inc(dve, 1)
                v.wait_ge(dve, own(dve))
                v.tensor_tensor(ex[:, :, :], ex[:, :, :], bx(den[:, :], TOPK), ALU.mult).then_inc(dve, 1)
                v.wait_ge(dve, own(dve))
                for k in range(TOPK):
                    ins = v.tensor_tensor(eq[:, k, :, :], ax(iota, NT), bx(idxf[:, :, k], NE), ALU.is_equal)
                ins.then_inc(dve, 1)
                v.wait_ge(dve, own(dve))
                for k in range(TOPK):
                    ins = v.tensor_tensor(eq[:, k, :, :], eq[:, k, :, :], bx(ex[:, :, k], NE), ALU.mult)
                ins.then_inc(dve, 1)
                v.wait_ge(dve, own(dve))
                for k in (0, 2):
                    ins = v.tensor_tensor(eq[:, k, :, :], eq[:, k, :, :], eq[:, k + 1, :, :], ALU.add)
                ins.then_inc(dve, 1)
                v.wait_ge(dve, own(dve))
                v.tensor_tensor(gates[:, :, :].rearrange("p e t -> p t e"), eq[:, 0, :, :], eq[:, 2, :, :], ALU.add)
        c.done({logits_done: 1, ready: 1, exps: 1})



def experts(c, h_hi, h_lo, gates, w_dram, acc):
    nc, count, own = c.nc, c.count, c.own
    banks = c.psum
    names = ["mx_load", "mx_whi", "mx_wlo", "mx_a", "mx_tanh", "mx_t1", "mx_s", "mx_hi", "mx_lo", "mx_y", "mx_acc"]
    names[0:1] = ["mx_load0", "mx_load1"]
    load0, load1, whi_done, wlo_done, a_done, tanh_done, t1_done, s_done, hi_done, lo_done, y_done, acc_done = (
        c.sem(x) for x in names)
    loaded = (load0, load1)
    with ExitStack() as ctx:
        ph = c.phase
        c.phase += 1
        sb = lambda name, shape, dt=F32: c.sb(f"{name}{ph}", shape, dt, ctx)
        raw = [sb(f"w_raw{i}", [P, 3, DK, HH]) for i in range(2)]
        whi = [sb(f"w_hi{i}", [P, 3, DK, HH], F32R) for i in range(2)]
        wlo = [sb(f"w_lo{i}", [P, 3, DK, HH], F32R) for i in range(2)]
        th = [sb(f"tanh{i}", [P, 512]) for i in range(2)]
        s1 = [sb(f"silu{i}", [P, 512]) for i in range(2)]
        s2 = [sb(f"hid{i}", [P, 512]) for i in range(2)]
        ahi = [sb(f"hid_hi{i}", [P, 2, 512], F32R) for i in range(2)]
        alo = [sb(f"hid_lo{i}", [P, 2, 512], F32R) for i in range(2)]
        gflat = gates[:, :, :].rearrange("p e t -> p (e t)")
        NH2 = 2 * NE

        def lp(it, k):
            return None if it is None else (it, k)

        def ok(q, it):
            return it is not None or 0 <= q < NH2

        def spans(eng, program, first):
            turns = NE // 2 - 2
            for q in range(-1, first):
                program(q, None)
            with eng.Fori(0, turns, 1) as it:
                for q in range(first, first + 4):
                    program(q, it)
            for q in range(first + 4 * turns, NH2):
                program(q, None)

        PASSES = ((0, 0), (0, 1), (1, 0))
        with nc.Block() as block:
            @block.sync
            def _(sp):
                w_d = w_dram.rearrange("e p n -> (e p) n")
                for e in range(2):
                    sp.dma_start(raw[e][:, :, :, :].rearrange("p a k n -> p (a k n)"), w_d[e * P:(e + 1) * P, :])\
                        .then_inc(loaded[e], 16)
                with sp.Fori(0, NE // 2 - 1, 1) as it:
                    for j in range(2):
                        sp.wait_ge(whi_done, count(whi_done, j + 1, (it, 2)))
                        sp.wait_ge(wlo_done, count(wlo_done, j + 1, (it, 2)))
                        sp.dma_start(raw[j][:, :, :, :].rearrange("p a k n -> p (a k n)"),
                                     w_d[bass.ds(it * (2 * P) + (j + 2) * P, P), :]).then_inc(loaded[j], 16)

            @block.tensor
            def _(pe):
                def program(q, it):
                    r = q + 1
                    if ok(r, it):
                        e, s = r // 2, r % 2
                        if s == 0:
                            pe.wait_ge(wlo_done, count(wlo_done, e + 1, lp(it, 2)))
                            pe.wait_ge(whi_done, count(whi_done, e + 1, lp(it, 2)))
                        W, H = (whi[e % 2], wlo[e % 2]), (h_hi, h_lo)
                        for m in range(2):
                            unit = 2 * r + m
                            if it is not None or unit >= 2:
                                pe.wait_ge(s_done, count(s_done, unit - 1, lp(it, 8)))
                            for mat in range(2):
                                for n, (k, (wp, hp)) in enumerate((k, ps) for k in range(DK) for ps in PASSES):
                                    ins = pe.matmul(banks[:, 2 * (unit % 2) + mat, :], W[wp][:, mat, k, m * P:(m + 1) * P],
                                                    H[hp][:, k, s * 512:(s + 1) * 512], start=n == 0, stop=n == 5)
                            ins.then_inc(a_done, 1)
                    if ok(q, it):
                        e, s = q // 2, q % 2
                        W, A = (whi[e % 2], wlo[e % 2]), (ahi[s], alo[s])
                        pe.wait_ge(hi_done, count(hi_done, 2 * q + 2, lp(it, 8)))
                        pe.wait_ge(lo_done, count(lo_done, 2 * q + 2, lp(it, 8)))
                        for j in range(4):
                            if j % 2 == 0 and (it is not None or q >= 2):
                                pe.wait_ge(acc_done, count(acc_done, 2 * (q - 2) + j // 2 + 1, lp(it, 8)))
                            for n, (k, (ap, wp)) in enumerate((k, ps) for k in range(DK) for ps in PASSES):
                                ins = pe.matmul(banks[:, 4 + 2 * s + j // 2, (j % 2) * D:(j % 2 + 1) * D],
                                                A[ap][:, k, j * P:(j + 1) * P], W[wp][:, 2, k, :],
                                                start=n == 0, stop=n == 5)
                            if j % 2:
                                ins.then_inc(y_done, 1)
                spans(pe, program, 3)

            @block.scalar
            def _(a):
                def split(e, it):
                    a.wait_ge(loaded[e % 2], count(loaded[e % 2], 16 * (e // 2 + 1), lp(it, 16)))
                    if it is not None or e >= 2:
                        a.wait_ge(y_done, count(y_done, 4 * (e - 1), lp(it, 8)))
                    a.activation(whi[e % 2][:, :, :, :], raw[e % 2][:, :, :, :], ACT.Copy).then_inc(whi_done, 1)

                def program(q, it):
                    if q < 0:
                        return split(0, None)
                    for m in range(2):
                        unit = 2 * q + m
                        a.wait_ge(a_done, count(a_done, unit + 1, lp(it, 8)))
                        if it is not None or unit >= 2:
                            a.wait_ge(t1_done, count(t1_done, unit - 1, lp(it, 8)))
                        a.activation(th[m][:, :], banks[:, 2 * m, :], ACT.Tanh, scale=0.5).then_inc(tanh_done, 1)
                        a.wait_ge(s_done, count(s_done, unit + 1, lp(it, 8)))
                        if it is not None or q >= 2:
                            a.wait_ge(y_done, count(y_done, 2 * (q - 1), lp(it, 8)))
                        a.activation(ahi[q % 2][:, m, :], s2[m][:, :], ACT.Copy).then_inc(hi_done, 1)
                    if q % 2 == 0 and (it is not None or q // 2 + 1 < NE):
                        split(q // 2 + 1, it)
                spans(a, program, 3)

            @block.vector
            def _(v):
                def program(q, it):
                    if q >= 0:
                        for m in range(2):
                            unit = 2 * q + m
                            v.wait_ge(tanh_done, count(tanh_done, unit + 1, lp(it, 8)))
                            if it is not None or unit >= 2:
                                v.wait_ge(s_done, count(s_done, unit - 1, lp(it, 8)))
                            v.scalar_tensor_tensor(out=s1[m][:, :], in0=th[m][:, :], scalar=1.0,
                                                   in1=banks[:, 2 * m, :], op0=ALU.add, op1=ALU.mult).then_inc(t1_done, 1)
                            v.wait_ge(t1_done, count(t1_done, unit + 1, lp(it, 8)))
                            if it is not None or unit >= 2:
                                v.wait_ge(lo_done, count(lo_done, unit - 1, lp(it, 8)))
                                v.wait_ge(hi_done, count(hi_done, unit - 1, lp(it, 8)))
                            v.scalar_tensor_tensor(out=s2[m][:, :], in0=s1[m][:, :], scalar=0.5,
                                                   in1=banks[:, 2 * m + 1, :], op0=ALU.mult, op1=ALU.mult).then_inc(s_done, 1)
                            v.wait_ge(hi_done, count(hi_done, unit + 1, lp(it, 8)))
                            if m == 0 and (it is not None or q >= 2):
                                v.wait_ge(y_done, count(y_done, 2 * (q - 1), lp(it, 8)))
                            v.tensor_tensor(alo[q % 2][:, m, :], s2[m][:, :],
                                            ahi[q % 2][:, m, :].bitcast(F32), ALU.subtract).then_inc(lo_done, 1)
                    p = q - 1
                    if ok(p, it):
                        add(p, it)

                def add(p, it):
                    e, s = p // 2, p % 2
                    for j in range(4):
                        t = 4 * s + j
                        if j % 2 == 0:
                            v.wait_ge(y_done, count(y_done, 2 * p + j // 2 + 1, lp(it, 8)))
                        if j == 0 and (it is not None or p >= 2):
                            v.wait_ge(acc_done, count(acc_done, 2 * (p - 1), lp(it, 8)))
                        gate = (gflat[:, e * NT + t:e * NT + t + 1] if it is None
                                else gflat[:, bass.ds(it * (2 * NT) + (e * NT + t), 1)])
                        ins = v.scalar_tensor_tensor(out=acc[:, t, :], scalar=gate, in1=acc[:, t, :],
                                                     in0=banks[:, 4 + 2 * s + j // 2, (j % 2) * D:(j % 2 + 1) * D],
                                                     op0=ALU.mult, op1=ALU.add)
                        if j % 2:
                            ins.then_inc(acc_done, 1)
                spans(v, program, 3)
                add(NH2 - 1, None)

            @block.gpsimd
            def _(g):
                def split(e, it):
                    g.wait_ge(whi_done, count(whi_done, e + 1, lp(it, 2)))
                    if it is not None or e >= 2:
                        g.wait_ge(y_done, count(y_done, 4 * (e - 1), lp(it, 8)))
                    g.tensor_tensor(wlo[e % 2][:, :, :, :], raw[e % 2][:, :, :, :],
                                    whi[e % 2][:, :, :, :].bitcast(F32), ALU.subtract).then_inc(wlo_done, 1)
                split(0, None)
                split(1, None)
                with g.Fori(0, NE // 2 - 1, 1) as it:
                    split(2, it)
                    split(3, it)
        c.done({load0: 8 * NE, load1: 8 * NE, whi_done: NE, wlo_done: NE, a_done: 4 * NE, tanh_done: 4 * NE, t1_done: 4 * NE,
                s_done: 4 * NE, hi_done: 4 * NE, lo_done: 4 * NE, y_done: 4 * NE, acc_done: 4 * NE})



class MambaMemory:
    def __init__(self, c, ctx):
        sb = lambda name, shape, dt=F32: c.sb("mb_" + name, shape, dt, ctx)
        self.hT = sb("hT", [P, DK, L])
        self.w_in = sb("w_in", [P, DK, 2 * INNER + 2 * DST + NH])
        self.w_out = sb("w_out", [P, NZ, D])
        self.cols = sb("cols", [P, 48])
        self.rows = sb("rows", [P, 3 * NH + D])
        self.scan = sb("scan", [P, 5 * P + CH])
        self.zT = sb("zT", [P, NZ, L])
        self.xT = sb("xT", [P, NZ, L])
        self.bcT = sb("bcT", [P, 2, L])
        self.btok = sb("btok", [P, NT, DST])
        self.xd = sb("xd", [P, NT, INNER])
        self.dA = sb("dA", [P, NT * NH])
        self.rev = sb("rev", [P, NT * NH])
        self.tot = sb("tot", [P, 2, NT * NH])
        self.head = sb("head", [CH, 2, NT * NH])
        self.b_z, self.b_x = self.cols[:, 0:4], self.cols[:, 4:10]
        self.conv_w = self.cols[:, 10:34].rearrange("p (m j) -> p m j", j=TAPS)
        self.conv_b = self.cols[:, 34:40]
        self.d_col, self.norm_w = self.cols[:, 40:44], self.cols[:, 44:48]
        self.later = self.scan[:, 0:P]
        self.upto = self.scan[:, P:2 * P].rearrange("p (c l) -> p c l", c=2)
        self.whole = self.scan[:, 2 * P:4 * P].rearrange("p (c n) -> p c n", c=2)
        self.within = self.scan[:, 4 * P:4 * P + CH]
        self.ones = self.scan[:, 5 * P:5 * P + 1]


def mamba_front(c, m):
    nc, count, own = c.nc, c.count, c.own
    banks = c.psum
    with ExitStack() as ctx:
        sb = lambda name, shape, dt=F32: c.sb("mf_" + name, shape, dt, ctx)
        raw = [sb(f"raw{i}", [P, L + 4]) for i in range(2)]
        th = [sb(f"tanh{i}", [P, L]) for i in range(2)]
        pre = [sb(f"pre{i}", [P, L]) for i in range(2)]
        dt = sb("dt", [P, NT, NH])
        arow = sb("arow", [P, NH])
        dtb = sb("dtb", [P, NH])
        half = sb("half", [P, 10])
        names = ["mf_dt", "mf_dtb", "mf_sp", "mf_dtok", "mf_sum", "mf_dec", "mf_pj", "mf_pre", "mf_half", "mf_conv",
                 "mf_th", "mf_out", "mf_tr", "mf_trev", "mf_arow", "mf_acc", "mf_bev"]
        (dt_mm, dt_in, softplus, dt_ok, sum_mm, decays, proj, pre_done, halved, conv_done, tanh_done, out_done,
         tr_done, tr_evac, arow_done, taps_done, b_evac) = (c.sem(x) for x in names)
        dve, act, pool = c.sem("dve_own"), c.sem("act_own"), c.sem("pool_own")
        z0, x0, dt0 = 0, INNER, INNER + CONVD
        NF = NZ + NX

        with nc.Block() as block:
            @block.tensor
            def _(pe):
                for t in range(NT):
                    for k in range(DK):
                        ins = pe.matmul(banks[:, 7, t * NH:(t + 1) * NH], m.hT[:, k, t * P:(t + 1) * P],
                                        m.w_in[:, k, dt0:dt0 + NH], start=k == 0, stop=k == DK - 1)
                ins.then_inc(dt_mm, 1)

                def project(f):
                    if f >= 2:
                        pe.wait_ge(pre_done, count(pre_done, 2 * (f - 1)))
                    for s in range(2):
                        for k in range(DK):
                            ins = pe.matmul(banks[:, 2 * (f % 2) + s, :], m.w_in[:, k, f * P:(f + 1) * P],
                                            m.hT[:, k, s * 512:(s + 1) * 512], start=k == 0, stop=k == DK - 1)
                        ins.then_inc(proj, 1)

                def turn(f):
                    r = f - NZ
                    pe.wait_ge(out_done, count(out_done, f + 1))
                    src = m.xT[:, r, :] if r < NZ else m.bcT[:, 0, :]
                    for s in range(2):
                        if r:
                            pe.wait_ge(tr_evac, count(tr_evac, 2 * (r - 1) + s + 1))
                        for j in range(4):
                            ins = pe.transpose(banks[:, 4 + s, j * P:(j + 1) * P],
                                               src[:, (4 * s + j) * P:(4 * s + j + 1) * P], c.ident[:, :])
                        ins.then_inc(tr_done, 1)

                for f in range(NF):
                    project(f)
                    if f == 1:
                        pe.wait_ge(dt_ok, count(dt_ok, 1))
                        for n in range(5):
                            lhs, rows = ((m.upto[:, 0, :], CH), (m.upto[:, 1, :], CH), (m.later, P),
                                         (m.whole[:, 0, :], P), (m.whole[:, 1, :], P))[n]
                            if n:
                                pe.wait_ge(decays, count(decays, n))
                            pe.matmul(banks[0:rows, 6, :], lhs, m.dA[:, :], start=True, stop=True).then_inc(sum_mm, 1)
                    if f >= NZ + 2 and f - 2 < NF - 1:
                        turn(f - 2)
                turn(NF - 2)

            @block.scalar
            def _(a):
                a.activation(arow[:, :], m.rows[:, 2 * NH:3 * NH], ACT.Exp).then_inc(arow_done, 1)
                a.wait_ge(dt_in, count(dt_in, 1))
                a.activation(dt[:, :, :], dt[:, :, :], ACT.Exp).then_inc(act, 1)
                a.wait_ge(act, own(act))
                a.activation(dt[:, :, :], dt[:, :, :], ACT.Ln, bias=1.0).then_inc(softplus, 1)
                a.wait_ge(halved, count(halved, 1))

                def pre_of(f):
                    for s in range(2):
                        a.wait_ge(proj, count(proj, 2 * f + s + 1))
                        if f >= 2 and s == 0:
                            a.wait_ge(out_done, count(out_done, f - 1))
                        if f < NZ:
                            ins = a.activation(pre[f % 2][:, s * 512:(s + 1) * 512], banks[:, 2 * (f % 2) + s, :],
                                               ACT.Identity, bias=half[:, f:f + 1], scale=0.5)
                        else:
                            ins = a.activation(raw[f % 2][:, 3 + s * 512:3 + (s + 1) * 512],
                                               banks[:, 2 * (f % 2) + s, :], ACT.Identity,
                                               bias=m.b_x[:, f - NZ:f - NZ + 1], scale=1.0)
                        ins.then_inc(pre_done, 1)

                def tanh_of(f):
                    if f < NZ:
                        a.wait_ge(pre_done, count(pre_done, 2 * f + 2))
                    else:
                        a.wait_ge(conv_done, count(conv_done, f - NZ + 1))
                    a.activation(th[f % 2][:, :], pre[f % 2][:, :], ACT.Tanh).then_inc(tanh_done, 1)

                pre_of(0)
                for f in range(NF):
                    if f == 1:
                        for n, dst in enumerate((m.head[:, 0, :], m.head[:, 1, :], m.rev[:, :], m.tot[:, 0, :],
                                                 m.tot[:, 1, :])):
                            a.wait_ge(sum_mm, count(sum_mm, n + 1))
                            a.activation(dst, banks[0:dst.shape[0], 6, :], ACT.Exp).then_inc(decays, 1)
                    if f + 1 < NF and f + 1 < NZ:
                        tanh_of(f)
                        pre_of(f + 1)
                    else:
                        if f + 1 < NF:
                            pre_of(f + 1)
                        tanh_of(f)
                for s in range(2):
                    a.wait_ge(tr_done, count(tr_done, 2 * NZ + s + 1))
                    a.activation(m.btok[:, 4 * s:4 * s + 4, :].rearrange("p t n -> p (t n)"),
                                  banks[:, 4 + s, :], ACT.Copy).then_inc(b_evac, 1)

            @block.gpsimd
            def _(g):
                g.tensor_tensor(c.x[:, :, :], c.x[:, :, :], ax(m.rows[:, 3 * NH:3 * NH + D], NT), ALU.add)
                for i in range(2):
                    g.memset(raw[i][:, 0:3], 0.0)
                for j in range(NZ):
                    g.tensor_scalar(m.w_out[:, j, :], m.w_out[:, j, :], m.norm_w[:, j:j + 1], None, ALU.mult)
                g.memset(half[:, 9:10], 0.0).then_inc(pool, 1)
                g.wait_ge(pool, own(pool))
                g.nop().then_inc(taps_done, 1)

            @block.vector
            def _(v):
                v.tensor_scalar(half[:, 0:NZ], m.b_z, 0.5, None, ALU.mult)
                v.tensor_scalar(m.cols[:, 10:40], m.cols[:, 10:40], 0.5, None, ALU.mult).then_inc(halved, 1)
                v.tensor_tensor(dtb[:, :], m.rows[:, 0:NH], m.rows[:, NH:2 * NH], ALU.add).then_inc(dve, 1)
                v.wait_ge(dve, own(dve))
                v.wait_ge(dt_mm, count(dt_mm, 1))
                v.tensor_tensor(dt[:, :, :], banks[:, 7, :].rearrange("p (t h) -> p t h", t=NT),
                                ax(dtb[:, :], NT), ALU.add).then_inc(dve, 1)
                v.wait_ge(dve, own(dve))
                v.tensor_scalar(dt[:, :, :], dt[:, :, :], 20.0, None, ALU.min).then_inc(dt_in, 1)
                v.wait_ge(softplus, count(softplus, 1))
                v.wait_ge(arow_done, count(arow_done, 1))
                v.tensor_scalar(dt[:, :, :], dt[:, :, :], 0.001, 0.1, ALU.max, ALU.min).then_inc(dve, 1)
                v.wait_ge(dve, own(dve))
                v.tensor_scalar(arow[:, :], arow[:, :], -1.0, None, ALU.mult).then_inc(dve, 1)
                v.wait_ge(dve, own(dve))
                v.tensor_tensor(m.dA[:, :].rearrange("p (t h) -> p t h", t=NT), dt[:, :, :],
                                ax(arow[:, :], NT), ALU.mult).then_inc(dt_ok, 1)
                v.wait_ge(taps_done, count(taps_done, 1))

                def gate_of(f):
                    dst = m.zT[:, f, :] if f < NZ else m.xT[:, f - NZ, :] if f < 2 * NZ else m.bcT[:, f - 2 * NZ, :]
                    v.wait_ge(tanh_done, count(tanh_done, f + 1))
                    v.scalar_tensor_tensor(out=dst, in0=th[f % 2][:, :], scalar=1.0,
                                           in1=pre[f % 2][:, :], op0=ALU.add, op1=ALU.mult).then_inc(out_done, 1)

                def evac_of(f):
                    r = f - NZ
                    for s in range(2):
                        v.wait_ge(tr_done, count(tr_done, 2 * r + s + 1))
                        out = m.xd[:, 4 * s:4 * s + 4, r * P:(r + 1) * P].rearrange("p t (h q) -> p t h q", q=HP)
                        v.tensor_tensor(out, banks[:, 4 + s, :].rearrange("p (t h q) -> p t h q", t=4, q=HP),
                                        bx(dt[:, 4 * s:4 * s + 4, r * 16:(r + 1) * 16], HP), ALU.mult).then_inc(tr_evac, 1)

                for f in range(NF):
                    if f >= NZ:
                        r = f - NZ
                        v.wait_ge(pre_done, count(pre_done, 2 * f + 2))
                        src, dst = raw[f % 2], pre[f % 2][:, :]
                        if r == 0:
                            v.wait_ge(out_done, count(out_done, f))
                        v.tensor_scalar(dst, src[:, 3:3 + L], m.conv_w[:, r, 3:4], m.conv_b[:, r:r + 1],
                                        ALU.mult, ALU.add).then_inc(dve, 1)
                        v.wait_ge(dve, own(dve))
                        for j in range(3):
                            ins = v.scalar_tensor_tensor(out=dst, in0=src[:, j:j + L], scalar=m.conv_w[:, r, j:j + 1],
                                                         in1=dst, op0=ALU.mult, op1=ALU.add)
                            if j < 2:
                                ins.then_inc(dve, 1)
                                v.wait_ge(dve, own(dve))
                        ins.then_inc(conv_done, 1)
                    gate_of(f)
                    if f >= NZ + 2 and f - 2 < 2 * NZ:
                        evac_of(f - 2)
        c.done({dt_mm: 1, dt_in: 1, softplus: 1, dt_ok: 1, sum_mm: 5, decays: 5, proj: 2 * NF, pre_done: 2 * NF,
                halved: 1, conv_done: NX, tanh_done: NF, out_done: NF, tr_done: 2 * NZ + 2, tr_evac: 2 * NZ, b_evac: 2,
                arow_done: 1, taps_done: 1})


def mamba_scan(c, m):
    nc, count, own = c.nc, c.count, c.own
    banks = c.psum
    diag = banks[0:CH, 2:4, :].rearrange("p b n -> p (b n)")
    shared = banks[:, 7, :]
    names = ["ms_stage", "ms_xdb", "ms_xdr", "ms_g", "ms_gm", "ms_rb", "ms_seg", "ms_l", "ms_m", "ms_yd", "ms_off",
             "ms_st", "ms_tmp", "ms_upd", "ms_y1", "ms_y", "ms_t", "ms_yt", "ms_gz", "ms_sq", "ms_out", "ms_var",
             "ms_pow", "ms_x", "ms_init"]
    (stage_done, xdb_done, xdr_done, g_done, gm_done, rb_done, seg_done, l_done, m_done, yd_done, off_done, st_done,
     tmp_done, upd_done, y1_done, y_done, t_done, yt_done, gz_done, sq_done, out_done, var_done, pow_done, x_done,
     init_done) = (c.sem(x) for x in names)
    per = {s: 1 for s in (stage_done, xdb_done, xdr_done, g_done, gm_done, y1_done, y_done, t_done, yt_done, gz_done,
                          sq_done, out_done, var_done, pow_done, x_done)}
    per.update({s: 8 for s in (rb_done, seg_done, l_done, m_done, yd_done)})
    per.update({s: 2 for s in (off_done, st_done, tmp_done, upd_done)})
    NG = NH // 8
    with ExitStack() as ctx:
        sb = lambda name, shape, dt=F32: c.sb("ms_" + name, shape, dt, ctx)
        bcs = [sb(f"bc{i}", [P, 2, P]) for i in range(2)]
        bts = [sb(f"bt{i}", [P, DST]) for i in range(2)]
        xdb = [sb(f"xdb{i}", [P, NH, 2, HP]) for i in range(2)]
        xdr = [sb(f"xdr{i}", [P, INNER]) for i in range(2)]
        gm = [sb(f"gm{i}", [P, CH]) for i in range(2)]
        rbuf = [sb(f"rb{i}", [P, 8, CH]) for i in range(2)]
        lbuf = [sb(f"l{i}", [P, 8, CH]) for i in range(2)]
        mbuf = [sb(f"m{i}", [P, 8, CH]) for i in range(2)]
        state = [sb(f"state{i}", [P, INNER]) for i in range(2)]
        tmp = sb("tmp", [P, INNER])
        ysb = sb("y", [CH, 2, INNER])
        yT = sb("yT", [P, NZ, P])
        gz = sb("gz", [P, NZ, P])
        sq = sb("sq", [P, NZ, P])
        var = sb("var", [P, 4])
        x_flat = c.x[:, :, :].rearrange("p t d -> p (t d)")
        xd_flat = m.xd[:, :, :].rearrange("p t n -> p (t n)")
        bt_flat = m.btok[:, :, :].rearrange("p t n -> p (t n)")

        def real(n, it):
            return it is not None or 0 <= n < NT

        def at(sem, n, j=1, it=None):
            k = per[sem]
            return count(sem, k * n + j, None if it is None else (it, 2 * k))

        def tile(n, width, it):
            return slice(n * width, (n + 1) * width) if it is None else bass.ds(it * (2 * width) + n * width, width)

        def spans(eng, program):
            for n in (-1, 0, 1):
                program(n, None)
            with eng.Fori(0, NT // 2 - 2, 1) as it:
                for n in (2, 3):
                    program(n, it)
            for n in range(NT - 2, NT + 1):
                program(n, None)

        def back(n, g, k):
            return (n, g - k) if g >= k else (n - 1, g - k + NG)

        with nc.Block() as block:
            @block.tensor
            def _(pe):
                def step(n, it):
                    for g in range(NG):
                        if real(n, it):
                            pe.wait_ge(rb_done, at(rb_done, n, g + 1, it))
                            n2, g2 = back(n, g, 2)
                            if real(n2, it):
                                pe.wait_ge(l_done, at(l_done, n2, g2 + 1, it))
                            pe.matmul(banks[:, g % 2, :], m.later,
                                      rbuf[g % 2][:, :, :].rearrange("p h l -> p (h l)"),
                                      start=True, stop=True).then_inc(seg_done, 1)
                        if g == 1 and real(n + 1, it):
                            if real(n - 2, it):
                                pe.wait_ge(x_done, at(x_done, n - 2, 1, it))
                            elif real(n, it):
                                pe.wait_ge(gm_done, at(gm_done, n, 1, it))
                            pe.wait_ge(stage_done, at(stage_done, n + 1, 1, it))
                            bc = bcs[(n + 1) % 2]
                            pe.matmul(shared[:, 0:P], bc[:, 0, :], bc[:, 1, :], start=True, stop=True).then_inc(g_done, 1)
                        if g in (4, 7) and real(n, it):
                            j = int(g == 7)
                            if g == 4:
                                pe.wait_ge(stage_done, at(stage_done, n, 1, it))
                                if real(n + 1, it):
                                    pe.wait_ge(gm_done, at(gm_done, n + 1, 1, it))
                                pe.wait_ge(xdr_done, at(xdr_done, n, 1, it))
                                if real(n - 1, it):
                                    pe.wait_ge(y_done, at(y_done, n - 1, 1, it))
                                    pe.wait_ge(upd_done, at(upd_done, n - 1, 2, it))
                                else:
                                    pe.wait_ge(init_done, count(init_done, 1))
                            else:
                                pe.wait_ge(upd_done, at(upd_done, n, 1, it))
                            pe.matmul(banks[0:CH, 4 + j, :], bcs[n % 2][:, 1, j * CH:(j + 1) * CH],
                                      state[j][:, :], start=True, stop=True).then_inc(off_done, 1)
                            pe.matmul(banks[:, 6, :], bts[n % 2][j * CH:(j + 1) * CH, :],
                                      xdr[n % 2][j * CH:(j + 1) * CH, :], start=True, stop=True).then_inc(st_done, 1)
                        if g == 4 and real(n - 1, it):
                            if it is None:
                                pe.wait_ge(y_done, at(y_done, n - 1, 1, it))
                                if not real(n + 1, it):
                                    pe.wait_ge(x_done, at(x_done, n - 2, 1, it))
                            for ch in range(2):
                                for j in range(NZ):
                                    ins = pe.transpose(shared[:, j * P + ch * CH:j * P + (ch + 1) * CH],
                                                       ysb[:, ch, j * P:(j + 1) * P], c.ident[0:CH, 0:CH])
                            ins.then_inc(t_done, 1)
                        if g == 6 and real(n - 1, it):
                            pe.wait_ge(sq_done, at(sq_done, n - 1, 1, it))
                            pe.wait_ge(gz_done, at(gz_done, n - 1, 1, it))
                            for j in range(NZ):
                                pe.matmul(shared[:, D:D + 1], sq[:, j, :], m.ones, start=j == 0, stop=j == NZ - 1)
                            for j in range(NZ):
                                ins = pe.matmul(shared[:, 0:D], gz[:, j, :], m.w_out[:, j, :],
                                                start=j == 0, stop=j == NZ - 1)
                            ins.then_inc(out_done, 1)
                        n2, g2 = back(n, g, 2)
                        if real(n2, it):
                            pe.wait_ge(m_done, at(m_done, n2, g2 + 1, it))
                            if g2 == 0:
                                pe.wait_ge(xdb_done, at(xdb_done, n2, 1, it))
                                if real(n2 - 1, it):
                                    pe.wait_ge(y_done, at(y_done, n2 - 1, 1, it))
                            for h in range(8):
                                hh = 8 * g2 + h
                                ins = pe.matmul(diag[:, hh * 16:(hh + 1) * 16], mbuf[g2 % 2][:, h, :],
                                                xdb[n2 % 2][:, hh, :, :].rearrange("p c q -> p (c q)"),
                                                start=True, stop=True)
                            ins.then_inc(yd_done, 1)
                spans(pe, step)

            @block.scalar
            def _(a):
                def step(n, it):
                    for g in range(NG):
                        if g == 0 and real(n + 1, it):
                            k = n + 1
                            if real(n - 1, it):
                                a.wait_ge(st_done, at(st_done, n - 1, 2, it))
                            a.activation(bcs[k % 2][:, :, :], m.bcT[:, :, tile(k, P, it)], ACT.Copy)
                            a.activation(bts[k % 2][:, :], bt_flat[:, tile(k, P, it)], ACT.Copy).then_inc(stage_done, 1)
                        if g == 2 and real(n + 1, it):
                            k = n + 1
                            if real(n - 1, it):
                                a.wait_ge(yd_done, at(yd_done, n - 1, 8, it))
                            else:
                                a.wait_ge(init_done, count(init_done, 1))
                            for ch in range(2):
                                rows = slice(ch * CH, (ch + 1) * CH)
                                ins = a.activation(xdb[k % 2][rows, :, ch, :], xd_flat[rows, tile(k, INNER, it)]
                                                   .rearrange("p (h q) -> p h q", q=HP), ACT.Copy)
                            ins.then_inc(xdb_done, 1)
                        if real(n, it):
                            a.wait_ge(seg_done, at(seg_done, n, g + 1, it))
                            n2, g2 = back(n, g, 2)
                            if real(n2, it):
                                a.wait_ge(m_done, at(m_done, n2, g2 + 1, it))
                            a.activation(lbuf[g % 2][:, :, :].rearrange("p h l -> p (h l)"),
                                         banks[:, g % 2, :], ACT.Exp).then_inc(l_done, 1)
                        if g == 5 and real(n - 1, it):
                            a.wait_ge(gz_done, at(gz_done, n - 1, 1, it))
                            if real(n - 2, it):
                                a.wait_ge(out_done, at(out_done, n - 2, 1, it))
                            a.activation(sq[:, :, :], gz[:, :, :], ACT.Square).then_inc(sq_done, 1)
                spans(a, step)

            @block.gpsimd
            def _(q):
                q.memset(state[0][:, :], 0.0)
                for i in range(2):
                    q.memset(xdb[i][:, :, :, :], 0.0)
                q.memset(var[:, 3:4], -0.5).then_inc(init_done, 1)

                def step(n, it):
                    for g in range(NG):
                        k, gk = (n, g + 2) if g + 2 < NG else (n + 1, g + 2 - NG)
                        if real(k, it):
                            if real(n, it):
                                q.wait_ge(seg_done, at(seg_done, n, g + 1, it))
                            d = (m.dA[:, 8 * NG * k + 8 * gk:8 * NG * k + 8 * gk + 8] if it is None
                                 else m.dA[:, bass.ds(it * (2 * NH) + (NH * k + 8 * gk), 8)])
                            q.tensor_tensor(rbuf[gk % 2][:, :, :], bx(d, CH), ax(m.within, 8), ALU.mult).then_inc(rb_done, 1)
                        if g == 6 and real(n - 1, it):
                            q.wait_ge(var_done, at(var_done, n - 1, 1, it))
                            q.wait_ge(init_done, count(init_done, 1))
                            q.tensor_tensor(var[:, 1:2], var[:, 0:1], var[:, 3:4], ALU.pow).then_inc(pow_done, 1)
                spans(q, step)

            @block.vector
            def _(v):
                def step(n, it):
                    for g in range(NG):
                        n1, g1 = back(n, g, 1)
                        if real(n1, it):
                            v.wait_ge(l_done, at(l_done, n1, g1 + 1, it))
                            if g1 == 0:
                                v.wait_ge(gm_done, at(gm_done, n1, 1, it))
                            n3, g3 = back(n, g, 3)
                            if real(n3, it):
                                v.wait_ge(yd_done, at(yd_done, n3, g3 + 1, it))
                            v.tensor_tensor(mbuf[g1 % 2][:, :, :], lbuf[g1 % 2][:, :, :],
                                            ax(gm[n1 % 2][:, :], 8), ALU.mult).then_inc(m_done, 1)
                        if g == 0 and real(n + 1, it):
                            k = n + 1
                            if real(n - 1, it):
                                v.wait_ge(st_done, at(st_done, n - 1, 2, it))
                            v.tensor_tensor(
                   xdr[k % 2][:, :].rearrange("p (h q) -> p h q", q=HP),
                   xd_flat[:, tile(k, INNER, it)].rearrange("p (h q) -> p h q", q=HP),
                   bx(m.rev[:, tile(k, NH, it)], HP), ALU.mult).then_inc(xdr_done, 1)
                        if g == 2 and real(n + 1, it):
                            k = n + 1
                            v.wait_ge(g_done, at(g_done, k, 1, it))
                            if real(n - 1, it):
                                v.wait_ge(m_done, at(m_done, n - 1, 8, it))
                            for ch in range(2):
                                rows = slice(ch * CH, (ch + 1) * CH)
                                ins = v.tensor_tensor(gm[k % 2][rows, :], shared[rows, rows], m.within[rows, :],
                                                      ALU.mult)
                            ins.then_inc(gm_done, 1)
                        if g == 2 and real(n - 1, it):
                            k = n - 1
                            v.wait_ge(off_done, at(off_done, k, 2, it))
                            if real(n - 2, it):
                                v.wait_ge(t_done, at(t_done, n - 2, 1, it))
                            for ch in range(2):
                                ins = v.tensor_tensor(ysb[:, ch, :].rearrange("p (h q) -> p h q", q=HP),
                                                      banks[0:CH, 4 + ch, :].rearrange("p (h q) -> p h q", q=HP),
                                                      bx(m.head[:, ch, tile(k, NH, it)], HP), ALU.mult)
                            ins.then_inc(y1_done, 1)
                            v.wait_ge(y1_done, at(y1_done, k, 1, it))
                            v.wait_ge(yd_done, at(yd_done, k, 8, it))
                            for ch in range(2):
                                y = ysb[:, ch, :].rearrange("p (h q) -> p h q", q=HP)
                                ins = v.tensor_tensor(y, y, diag.rearrange("p (h c q) -> p h c q", c=2, q=HP)[:, :, ch, :],
                                                      ALU.add)
                            ins.then_inc(y_done, 1)
                        if g in (5, 7) and real(n, it):
                            j = int(g == 7)
                            if n or j or it is not None:
                                v.wait_ge(upd_done, at(upd_done, n if j else n - 1, 1 if j else 2, it))
                            else:
                                v.wait_ge(init_done, count(init_done, 1))
                            v.tensor_tensor(tmp[:, :].rearrange("p (h q) -> p h q", q=HP),
                                            state[j][:, :].rearrange("p (h q) -> p h q", q=HP),
                                            bx(m.tot[:, j, tile(n, NH, it)], HP), ALU.mult).then_inc(tmp_done, 1)
                            v.wait_ge(tmp_done, at(tmp_done, n, j + 1, it))
                            v.wait_ge(st_done, at(st_done, n, j + 1, it))
                            v.tensor_tensor(state[1 - j][:, :], tmp[:, :], banks[:, 6, :], ALU.add).then_inc(upd_done, 1)
                        if g == 5 and real(n - 1, it):
                            k = n - 1
                            v.wait_ge(t_done, at(t_done, k, 1, it))
                            if real(n - 2, it):
                                v.wait_ge(out_done, at(out_done, n - 2, 1, it))
                            for j in range(NZ):
                                ins = v.scalar_tensor_tensor(out=yT[:, j, :], in0=m.xT[:, j, tile(k, P, it)],
                                                             scalar=m.d_col[:, j:j + 1],
                                                             in1=shared[:, j * P:(j + 1) * P],
                                                             op0=ALU.mult, op1=ALU.add)
                            ins.then_inc(yt_done, 1)
                            v.wait_ge(yt_done, at(yt_done, k, 1, it))
                            v.tensor_tensor(gz[:, :, :], yT[:, :, :], m.zT[:, :, tile(k, P, it)], ALU.mult).then_inc(gz_done, 1)
                        if g == 7 and real(n - 1, it):
                            k = n - 1
                            v.wait_ge(out_done, at(out_done, k, 1, it))
                            v.tensor_scalar(var[:, 0:1], shared[:, D:D + 1], 1.0 / INNER, 1e-6,
                                            ALU.mult, ALU.add).then_inc(var_done, 1)
                            v.wait_ge(pow_done, at(pow_done, k, 1, it))
                            xs = x_flat[:, tile(k, D, it)]
                            v.scalar_tensor_tensor(out=xs, in0=shared[:, 0:D], scalar=var[:, 1:2], in1=xs,
                                                   op0=ALU.mult, op1=ALU.add).then_inc(x_done, 1)
                spans(v, step)
        counts = {s: k * NT for s, k in per.items()}
        counts[init_done] = 1
        c.done(counts)



class AttentionWeights:

    def __init__(self, c, ctx, name, dram):
        self.wqkv = c.sb(name + "_wqkv", [P, DK, HKV * GW], F32, ctx)
        self.wo = c.sb(name + "_wo", [P, HQ * HD // P, D], F32, ctx)
        self.rope = c.sb(name + "_rope", [P, 2, NT, HD], F32, ctx)
        self.loaded = c.ctx.enter_context(c.nc.semaphore(name + "_loaded"))
        self.dram = [dram[name + "_wqkv"], dram[name + "_wo"], dram[name + "_rope"]]

    def load(self, eng):
        wqkv, wo, rope = self.dram
        eng.dma_start(self.wqkv[:, :, :], wqkv.rearrange("(k p) n -> p k n", p=P)).then_inc(self.loaded, 16)
        eng.dma_start(self.wo[:, :, :], wo.rearrange("(k p) n -> p k n", p=P)).then_inc(self.loaded, 16)
        eng.dma_start(self.rope[:, :, :, :], rope).then_inc(self.loaded, 16)

    def arrived(self, eng):
        eng.wait_ge(self.loaded, 48)


def add_residual(c, weights):
    with c.nc.Block() as block:
        @block.vector
        def _(v):
            v.tensor_tensor(c.x[:, :, :], c.x[:, :, :], c.u[:, :, :], ALU.add)

        @block.sync
        def _(sp):
            if weights is not None:
                weights.arrived(sp)


def hybrid_program(nc, d, out):
    with ExitStack() as ctx:
        c = Core(nc, ctx, d)
        ffn = AttentionWeights(c, ctx, "ffn", d)
        wg = c.sb("wg", [P, DK, NE])
        gates = c.sb("gates", [P, NE, NT])
        loads = ctx.enter_context(nc.semaphore("loads"))
        stored = ctx.enter_context(nc.semaphore("stored"))

        with ExitStack() as mctx:
            m = MambaMemory(c, mctx)
            with nc.Block() as block:
                @block.sync
                def _(sp):
                    sp.dma_start(c.x[:, :, :], d["x"].rearrange("(t p) d -> p t d", p=P)).then_inc(loads, 16)
                    sp.dma_start(c.ident[:, :], d["ident"]).then_inc(loads, 16)
                    sp.dma_start(c.consts[:, :], d["consts"]).then_inc(loads, 16)
                    sp.dma_start(m.w_in[:, :, :], d["w_in"].rearrange("(k p) n -> p k n", p=P)).then_inc(loads, 16)
                    sp.dma_start(m.cols[:, :], d["cols"]).then_inc(loads, 16)
                    sp.dma_start(m.rows[:, :], d["rows"].partition_broadcast(P)).then_inc(loads, 16)
                    sp.dma_start(m.scan[:, :], d["scan"]).then_inc(loads, 16)
                    sp.dma_start(m.w_out[:, :, :], d["w_out"].rearrange("(k p) n -> p k n", p=P)).then_inc(loads, 16)
                    sp.dma_start(wg[:, :, :], d["wg"].rearrange("(k p) n -> p k n", p=P)).then_inc(loads, 16)
                    sp.dma_start(c.ln_cols[:, :, :], d["ln_cols"]).then_inc(loads, 16)
                    ffn.load(sp)

                @block.vector
                def _(v):
                    v.wait_ge(loads, 160)
                    v.tensor_copy(c.ident16[:, :], c.ident[:, :])
                    v.tensor_copy(c.causal16[:, :], c.consts[:, P:2 * P])
            normalise(c, c.x, True, None, None, m.hT, c.u)
            mamba_front(c, m)
            mamba_scan(c, m)

        attn = AttentionWeights(c, ctx, "attn", d)
        hT = c.sb("hT", [P, DK, L])
        h_hi = c.sb("h_hi", [P, DK, L], F32R)
        h_lo = c.sb("h_lo", [P, DK, L], F32R)

        def feed_forward():
            normalise(c, c.x, True, 1e-5, c.ln_cols[:, 0, :], hT, c.u)
            attention(c, hT, ffn.wqkv, ffn.wo, ffn.rope, c.u)
            normalise(c, c.u, False, 1e-5, c.ln_cols[:, 1, :], hT, None, (h_hi, h_lo))
            router(c, hT, wg, gates)
            experts(c, h_hi, h_lo, gates, d["experts"], c.u)

        with nc.Block() as block:
            @block.sync
            def _(sp):
                attn.load(sp)
                ffn.arrived(sp)
        feed_forward()
        add_residual(c, attn)
        normalise(c, c.x, True, None, None, hT, c.u)
        attention(c, hT, attn.wqkv, attn.wo, attn.rope, c.x)
        feed_forward()
        add_residual(c, None)
        with nc.Block() as block:
            @block.sync
            def _(sp):
                sp.dma_start(out.rearrange("(t p) d -> p t d", p=P), c.x[:, :, :]).then_inc(stored, 16)
                sp.wait_ge(stored, 16)



def _rotary(base_exponents):
    ang = np.arange(L, dtype=np.float32)[:, None] * base_exponents[None, :]
    cos, sin = np.cos(ang), np.sin(ang)
    table = np.stack([np.concatenate([cos, cos], -1), np.concatenate([-sin, sin], -1)])
    return np.ascontiguousarray(table.reshape(2, NT, P, HD).transpose(2, 0, 1, 3))


def _grouped(wq, wk, wv):
    w = np.concatenate([wq.reshape(D, HKV, G * HD), wk.reshape(D, HKV, HD), wv.reshape(D, HKV, HD)], -1)
    return np.ascontiguousarray(w.reshape(D, HKV * GW))


def _scan_constants():
    t = np.arange(P)
    chunk, place = t // CH, t % CH
    later = (t[:, None] > t[None, :]) & (chunk[:, None] == chunk[None, :])
    upto = np.stack([(chunk[:, None] == k) & (place[:, None] <= np.arange(CH)[None, :]) for k in range(2)], 1)
    whole = np.stack([np.repeat((chunk == k)[:, None], P, 1) for k in range(2)], 1)
    within = place[:, None] <= np.arange(CH)[None, :]
    parts = [later, upto.reshape(P, -1), whole.reshape(P, -1), within, np.zeros((P, CH)), np.ones((P, CH))]
    return np.concatenate([np.asarray(p, np.float32) for p in parts], 1)


def kernel(**inputs):
    import concourse.bacc as bacc
    from concourse.bass_utils import run_bass_kernel_spmd

    a = {k: np.asarray(v) for k, v in inputs.items()}
    A, B, F = "L0_attn_a_", "L0_attn_b_", "L0_ffn_"
    cols = lambda v: v.reshape(-1, P).T
    b_in = a[A + "b_in"]
    split_b = INNER + CONVD
    taps = a[A + "conv_w"].reshape(TAPS, NX, P).transpose(2, 1, 0).reshape(P, NX * TAPS)
    halves = np.concatenate([np.arange(0, HD, 2), np.arange(1, HD, 2)])
    turned = lambda w: w.T.reshape(D, -1, HD)[:, :, halves].reshape(D, -1)
    place = np.arange(P)
    e32 = np.arange(HD // 2, dtype=np.float32)
    arrays = {
        "x": a[A + "x"].reshape(L, D),
        "ident": np.eye(P, dtype=np.float32),
        "consts": np.concatenate([np.tile(np.arange(P, dtype=np.float32), (P, 1)),
                                  np.where(place[:, None] >= place[None, :], 0.0, NEG).astype(np.float32)], 1),
        "w_in": a[A + "W_in"],
        "w_out": a[A + "W_out"],
        "cols": np.concatenate([cols(b_in[:split_b]), taps, cols(a[A + "conv_b"]),
                                cols(np.repeat(a[A + "D_param"], HP)), cols(a[A + "norm_w"])], 1),
        "rows": np.concatenate([b_in[split_b:], a[A + "dt_bias"], a[A + "A_log"], a[A + "b_out"]]),
        "scan": _scan_constants(),
        "wg": a[F + "wg"],
        "ln_cols": np.stack([cols(a[F + "ln_w"]), cols(a[F + "ff_ln_w"])], 1),
        "ffn_wqkv": _grouped(a[F + "wq"], a[F + "wk"], a[F + "wv"]),
        "ffn_wo": a[F + "wo"],
        "ffn_rope": _rotary(np.float32(1.0) / np.float32(150000.0) ** (e32 / np.float32(HD // 2))),
        "attn_wqkv": _grouped(turned(a[B + "Wq"]), turned(a[B + "Wk"]), a[B + "Wv"].T),
        "attn_wo": a[B + "Wo"].T,
        "attn_rope": _rotary(np.float32(1.0) / np.float32(10000.0) ** (e32 * np.float32(2) / np.float32(HD))),
        "experts": np.stack([a[F + "w1"], a[F + "w3"], a[F + "w2"]], 1).reshape(NE, 3, DK, P, HH)
                     .transpose(0, 3, 1, 2, 4).reshape(NE, P, 3 * DK * HH),
    }
    nc = bacc.Bacc("TRN2", target_bir_lowering=False, num_devices=1)
    d, feed = {}, {}
    for name, v in arrays.items():
        feed["in_" + name] = np.ascontiguousarray(v)
        d[name] = nc.dram_tensor("in_" + name, v.shape, F32, kind="ExternalInput").ap()
    out = nc.dram_tensor("out_dram", (L, D), F32, kind="ExternalOutput").ap()
    hybrid_program(nc, d, out)
    r = run_bass_kernel_spmd(nc, [feed], core_ids=[0])
    return r.results[0]["out_dram"].reshape(1, L, D)
```

```python
from contextlib import ExitStack

import numpy as np
import concourse.bass as bass
from concourse import mybir

F32 = mybir.dt.float32
F32R = mybir.dt.float32r
BF16 = mybir.dt.bfloat16
U32 = mybir.dt.uint32
ALU = mybir.AluOpType
ACT = mybir.ActivationFunctionType
AX = mybir.AxisListType

P = 128
L = 1024
D = 256
NT = L // P
DK = D // P
HQ, HKV, HD = 32, 8, 64
G = HQ // HKV
GW = (G + 2) * HD
STEPS = HKV * NT
BODY = 2 * NT
NE, TOPK, HH = 16, 4, 256
INNER, DST, NH, HP, TAPS = 512, 128, 64, 8, 4
CH = 64
CONVD = INNER + 2 * DST
NX = CONVD // P
NZ = INNER // P
NEG = -1.0e30


def ax(ap, n):
    return ap.unsqueeze(1).broadcast_to([ap.shape[0], n, ap.shape[1]])


def bx(ap, n):
    return ap.unsqueeze(len(ap.shape)).broadcast_to(list(ap.shape) + [n])


class Core:

    def __init__(self, nc, ctx, dram):
        self.nc, self.ctx, self.dram = nc, ctx, dram
        self.sems, self.before = {}, {}
        self.phase = 0
        sb = self.sb
        self.x = sb("x_res", [P, NT, D])
        self.u = sb("u_res", [P, NT, D])
        self.ident = sb("ident", [P, P])
        self.ident16 = sb("ident16", [P, P], BF16)
        self.causal16 = sb("causal16", [P, P], BF16)
        self.consts = sb("consts", [P, 256])
        self.ln_cols = sb("ln_cols", [P, 2, DK])
        self.psum = ctx.enter_context(nc.psum_tensor("banks", [P, 8, 512], F32))

    def sb(self, name, shape, dt=F32, ctx=None):
        return (ctx or self.ctx).enter_context(self.nc.sbuf_tensor(name, shape, dt))

    def sem(self, name):
        if name not in self.sems:
            self.sems[name] = self.ctx.enter_context(self.nc.semaphore(name))
            self.before[self.sems[name]] = 0
        return self.sems[name]

    def count(self, sem, n, loop=None):
        if loop is None:
            assert n >= 1
            return self.before[sem] + n
        return loop[0] * loop[1] + (self.before[sem] + n)

    def own(self, sem):
        self.before[sem] += 1
        return self.before[sem]

    def done(self, counts):
        for sem, n in counts.items():
            self.before[sem] += n



def normalise(c, src, layer, rms_eps, w_cols, hT, dst, splits=None, loads=None):
    nc, count, own = c.nc, c.count, c.own
    with ExitStack() as ctx:
        n = c.phase
        c.phase += 1
        cen = c.sb(f"nrm_cen{n}", [P, NT, D], ctx=ctx) if layer else src
        sq = c.sb(f"nrm_sq{n}", [P, NT, D], ctx=ctx)
        st = c.sb(f"nrm_st{n}", [P, 8, NT], ctx=ctx)
        mean, ssq, var, rstd, t0, r2 = (st[:, i, :] for i in range(6))
        hn = c.sb(f"nrm_h{n}", [P, NT, D], ctx=ctx) if rms_eps is not None else dst
        centred, squared, vard, rstdd, t0d, r2d = (
            c.sem(x) for x in ("nrm_centred", "nrm_squared", "nrm_var", "nrm_rstd", "nrm_t0", "nrm_r2"))
        normed, turned, evac, evac32 = (c.sem(x) for x in ("nrm_out", "nrm_turned", "nrm_evac", "nrm_evac32"))
        dve, pool = c.sem("dve_own"), c.sem("pool_own")
        banks = c.psum
        fused = layer and rms_eps is not None
        last_r = r2d if fused else rstdd

        with nc.Block() as block:
            @block.sync
            def _(sp):
                if loads is not None:
                    loads.load_first(sp)

            @block.vector
            def _(v):
                if layer:
                    v.tensor_reduce(mean, src[:, :, :], AX.X, ALU.add).then_inc(dve, 1)
                    v.wait_ge(dve, own(dve))
                    v.tensor_scalar(mean, mean, 1.0 / D, None, ALU.mult).then_inc(dve, 1)
                    v.wait_ge(dve, own(dve))
                    v.tensor_tensor(cen[:, :, :], src[:, :, :], bx(mean, D), ALU.subtract).then_inc(centred, 1)
                v.wait_ge(squared, count(squared, 1))
                v.tensor_reduce(ssq, sq[:, :, :], AX.X, ALU.add).then_inc(dve, 1)
                v.wait_ge(dve, own(dve))
                eps = 1e-5 if layer else rms_eps
                v.tensor_scalar(var, ssq, 1.0 / D, None, ALU.mult).then_inc(dve, 1)
                v.wait_ge(dve, own(dve))
                v.tensor_scalar(t0, var, eps, None, ALU.add).then_inc(vard, 1)
                v.wait_ge(rstdd, count(rstdd, 1))
                if fused:
                    v.tensor_tensor(var, var, rstd, ALU.mult).then_inc(dve, 1)
                    v.wait_ge(dve, own(dve))
                    v.tensor_tensor(var, var, rstd, ALU.mult).then_inc(dve, 1)
                    v.wait_ge(dve, own(dve))
                    v.tensor_scalar(t0, var, rms_eps, None, ALU.add).then_inc(t0d, 1)
                    v.wait_ge(r2d, count(r2d, 1))
                    v.tensor_tensor(r2, r2, rstd, ALU.mult).then_inc(dve, 1)
                    v.wait_ge(dve, own(dve))
                for k in range(DK):
                    v.tensor_tensor(hn[:, :, k * P:(k + 1) * P], cen[:, :, k * P:(k + 1) * P],
                                    bx(r2 if fused else rstd, P), ALU.mult).then_inc(normed, 1)
                if fused:
                    v.tensor_tensor(dst[:, :, :], cen[:, :, :], bx(rstd, D), ALU.mult)
                if splits:
                    hi, lo = splits
                    for b in range(2 * DK):
                        k, half = b // 2, b % 2
                        cols = slice(half * 512, half * 512 + 512)
                        v.wait_ge(evac, count(evac, b + 1))
                        v.tensor_tensor(lo[:, k, cols], hT[:, k, cols], hi[:, k, cols].bitcast(F32),
                                        ALU.subtract)

            @block.gpsimd
            def _(g):
                g.memset(st[:, 7, :], -0.5).then_inc(pool, 1)
                g.wait_ge(pool, own(pool))
                g.wait_ge(vard, count(vard, 1))
                g.tensor_tensor(rstd, t0, st[:, 7, :], ALU.pow).then_inc(rstdd, 1)
                if fused:
                    g.wait_ge(t0d, count(t0d, 1))
                    g.tensor_tensor(r2, t0, st[:, 7, :], ALU.pow).then_inc(r2d, 1)

            @block.scalar
            def _(a):
                if layer:
                    a.wait_ge(centred, count(centred, 1))
                a.activation(sq[:, :, :], cen[:, :, :], ACT.Square).then_inc(squared, 1)
                for b in range(2 * DK):
                    k, half = b // 2, b % 2
                    cols = slice(half * 512, half * 512 + 512)
                    a.wait_ge(turned, count(turned, b + 1))
                    if w_cols is None:
                        ins = a.activation(hT[:, k, cols], banks[:, b, :], ACT.Copy)
                    else:
                        ins = a.activation(hT[:, k, cols], banks[:, b, :], ACT.Copy, scale=w_cols[:, k:k + 1])
                    if splits:
                        ins.then_inc(evac32, 1)
                        a.wait_ge(evac32, count(evac32, b + 1))
                        ins = a.activation(splits[0][:, k, cols], hT[:, k, cols], ACT.Copy)
                    ins.then_inc(evac, 1)

            @block.tensor
            def _(t):
                for b in range(2 * DK):
                    k, half = b // 2, b % 2
                    t.wait_ge(normed, count(normed, k + 1))
                    for j in range(4):
                        ins = t.transpose(banks[:, b, j * P:(j + 1) * P],
                                          hn[:, half * 4 + j, k * P:(k + 1) * P], c.ident[:, :])
                    ins.then_inc(turned, 1)
        c.done({centred: int(layer), squared: 1, vard: 1, rstdd: 1, t0d: int(fused), r2d: int(fused),
                normed: DK, turned: 2 * DK, evac: 2 * DK, evac32: 2 * DK if splits else 0})



_TURN = ((0, 4), (0, 5), (1, 0), (0, 6), (1, 1), (0, 7), (1, 2), (1, 3))
GROUP_TILE = ([(0, t) for t in range(4)] + [(g + dg, t) for g in range(HKV - 1) for dg, t in _TURN]
              + [(HKV - 1, t) for t in range(4, NT)])
LATE_BEFORE = [sum(t >= 4 for _, t in GROUP_TILE[:n]) for n in range(len(GROUP_TILE))]
FIRST = 4

def attention(c, h_parts, w, acc):
    nc, count, own = c.nc, c.count, c.own
    banks = c.psum
    s_of = lambda h: banks[:, 2 * (h % 2):2 * (h % 2) + 2, :].rearrange("p b n -> p (b n)")
    pt = [banks[:, 4, :], banks[:, 5, :]]
    shared, o_ps, rec_ps = banks[:, 6, :], banks[:, 7, :], banks[:, 7, :]
    names = ["at_proj", "at_rope", "at_vhi", "at_vcopy", "at_split", "at_qt", "at_qtev", "at_kt", "at_ktev",
             "at_rt", "at_rtev", "at_s", "at_max", "at_exp", "at_t0", "at_t1", "at_phi0", "at_phi1", "at_plo",
             "at_pv", "at_norm", "at_op", "at_add", "at_rec", "at_sum", "at_hi", "at_ohi", "at_olo"]
    (proj_done, rope_done, v_hi_done, v_copied, split_done, qt_done, qt_evac, kt_done, kt_evac, rt_done, rt_evac,
     s_done, max_done, exp_done, t0_done, t1_done, phi0_done, phi1_done, plo_done, pv_done, norm_done, op_done,
     add_done, rec_done, sum_done, hi_done, ohi_done, olo_done) = (c.sem(x) for x in names)
    per_step = {s: 1 for s in (proj_done, rope_done, v_hi_done, v_copied, split_done, qt_done, qt_evac, kt_done,
                               kt_evac, rt_done, rt_evac, norm_done, op_done, add_done, rec_done, sum_done, pv_done, ohi_done, olo_done)}
    per_step.update({s: 4 for s in (s_done, max_done, exp_done, t0_done, phi0_done)})
    per_step[hi_done] = 2
    wqkv, wo, rope = w.parts[0], w.parts[1], w.rope
    PASSES = ((0, 0), (0, 1), (1, 0))

    with ExitStack() as ctx:
        ph = c.phase
        c.phase += 1
        sb = lambda name, shape, dt=F32: c.sb(f"{name}{ph}", shape, dt, ctx)
        ra = sb("rope_a", [P, 5, HD])
        rb = sb("rope_b", [P, 5, HD])
        rs = sb("rope_sum", [P, 5, HD])
        qk = [sb(f"qk_parts{i}", [P, 6, P], F32R) for i in range(2)]
        qT = [sb(f"qT{i}", [P, G, P], F32R) for i in range(2)]
        kT = [sb(f"kT{i}", [P, 2, L], F32R) for i in range(2)]
        vv = [sb(f"v{i}", [P, NT, 3, HD], F32R) for i in range(2)]
        prob = [sb(f"prob{i}", [P, L]) for i in range(2)]
        pT_hi, pT_lo = ([sb(f"pT_{x}{i}", [P, NT, G, P], F32R) for i in range(2)] for x in ("hi", "lo"))
        nmax = sb("nmax", [P, 4])
        sums = sb("sums", [P, 2, G])
        rec = sb("rec", [P, 2, G])
        rec_rows = sb("rec_rows", [P, G * P])
        oT = sb("oT", [P, G, P])
        oT_parts = [sb(f"oT_{part}", [P, G, P], F32R) for part in ("hi", "lo")]

        group, tile = (lambda n: GROUP_TILE[n % STEPS][0]), (lambda n: GROUP_TILE[n % STEPS][1])

        def real(n, it):
            return it is not None or 0 <= n < STEPS

        def at(sem, n, j=1, it=None):
            k = per_step[sem]
            return count(sem, k * n + j, None if it is None else (it, k * BODY))

        def at_late(sem, n, h, it):
            k = 4 * LATE_BEFORE[n] + h + 1
            return count(sem, k, None if it is None else (it, 32))

        def at_lo(n, h, chunk, it):
            per_head = 2 if tile(n) >= 4 else 1
            k = 4 * n + 4 * LATE_BEFORE[n] + per_head * h + chunk + 1
            return count(plo_done, k, None if it is None else (it, 4 * BODY + 32))

        def chunks(n, h):
            t = tile(n)
            return [(h % 2, t + 1)] if t < 4 else [(0, 4), (1, t - 3)]

        def last_user(n, h, bank):
            while (n, h) > (0, 0):
                n, h = (n, h - 1) if h else (n - 1, 3)
                for chunk, (b, _) in reversed(list(enumerate(chunks(n, h)))):
                    if b == bank:
                        return n, h, chunk
            return None

        def spans(eng, program):
            loops = STEPS // BODY - 1
            for n in range(-2, FIRST):
                program(n, None)
            with eng.Fori(0, loops, 1) as it:
                for n in range(FIRST, FIRST + BODY):
                    program(n, it)
            for n in range(FIRST + BODY * loops, STEPS + 2):
                program(n, None)

        def split_group(n, t, it):
            if real(n, it) and tile(n) == t and (it is not None or group(n) + 1 < HKV):
                return group(n) + 1
            return None

        def turned(b, tiles):
            return pt[b][:, 0:tiles * P].rearrange("p (j n) -> p j n", j=tiles)

        def two_back(n, h):
            return (n, h - 2) if h >= 2 else (n - 1, h + 2)

        with nc.Block() as block:
            @block.tensor
            def _(pe):
                def step(n, it):
                    for h in range(G):
                        n2, h2 = two_back(n, h)
                        i2 = (4 * n2 + h2) % 2

                        if real(n2, it):
                            pe.wait_ge(exp_done, at(exp_done, n2, h2 + 1, it))
                            for chunk, (bank, blocks) in enumerate(chunks(n2, h2)):
                                user = last_user(n2, h2, bank)
                                if user:
                                    pe.wait_ge(plo_done, at_lo(*user, it))
                                for j in range(blocks):
                                    jj = 4 * chunk + j
                                    ins = pe.transpose(pt[bank][:, j * P:(j + 1) * P],
                                                       prob[i2][:, jj * P:(jj + 1) * P], c.ident[:, :])
                                ins.then_inc(t1_done if chunk else t0_done, 1)
                        if real(n, it):
                            t, par = tile(n), group(n) % 2
                            if h == 0:
                                pe.wait_ge(qt_evac, at(qt_evac, n, 1, it))
                                pe.wait_ge(kt_evac, at(kt_evac, n, 1, it))
                            s_ps, width = s_of(h), (t + 1) * P
                            for lo in range(0, width, 512):
                                hi = min(lo + 512, width)
                                for part in range(2):
                                    pe.matmul(s_ps[:, lo:hi], qT[n % 2][:, h, :], kT[par][:, part, lo:hi],
                                              start=part == 0, stop=part == 1 and hi < width)
                            pe.matmul(s_ps[:, width - P:width], c.ident16[:, :], c.causal16[:, :],
                                      start=False, stop=True).then_inc(s_done, 1)
                        if h == 0 and real(n + 2, it):
                            m = n + 2
                            t = tile(m)
                            if tile(m) == 0:
                                pe.wait_ge(w.lo_done[0], w.at(w.lo_done[0], group(m), 1, it))
                            if real(n - 3, it):
                                pe.wait_ge(add_done, at(add_done, n - 3, 1, it))
                            elif real(n + 1, it):
                                pe.wait_ge(v_copied, at(v_copied, n + 1, 1, it))
                            for i, (k, (hp, wp)) in enumerate((k, ps) for k in range(DK) for ps in PASSES):
                                ins = pe.matmul(shared[:, 0:GW], h_parts[hp][:, k, t * P:(t + 1) * P],
                                                wqkv[group(m) % 2][wp][:, k, :], start=i == 0, stop=i == 3 * DK - 1)
                            ins.then_inc(proj_done, 1)
                        if h == 1 and real(n + 1, it):
                            if real(n + 2, it):
                                pe.wait_ge(v_copied, at(v_copied, n + 2, 1, it))
                            elif real(n - 3, it):
                                pe.wait_ge(add_done, at(add_done, n - 3, 1, it))
                            pe.wait_ge(split_done, at(split_done, n + 1, 1, it))
                            for q in range(G):
                                ins = pe.transpose(shared[:, q * P:(q + 1) * P],
                                                   qk[(n + 1) % 2][:, q, :].bitcast(F32), c.ident[:, :])
                            ins.then_inc(qt_done, 1)
                        if h == 2 and real(n + 1, it):
                            pe.wait_ge(qt_evac, at(qt_evac, n + 1, 1, it))
                            for q in range(2):
                                ins = pe.transpose(shared[:, q * P:(q + 1) * P],
                                                   qk[(n + 1) % 2][:, 4 + q, :].bitcast(F32), c.ident[:, :])
                            ins.then_inc(kt_done, 1)
                        if h == 2 and real(n - 1, it):
                            m = n - 1
                            pe.wait_ge(rec_done, at(rec_done, m, 1, it))
                            if real(m - 1, it):
                                pe.wait_ge(norm_done, at(norm_done, m - 1, 1, it))
                            for q in range(G):
                                ins = pe.transpose(rec_ps[:, q * P:(q + 1) * P],
                                                   rec[:, m % 2, q:q + 1].broadcast_to([P, P]), c.ident[:, :])
                            ins.then_inc(rt_done, 1)
                        m = n - 1 if h == 3 else n - 2
                        if h in (0, 3) and real(m, it):
                            V, last = vv[group(m) % 2], tile(m)
                            half = last // 4 + 1
                            if h == 3:
                                pe.wait_ge(plo_done, at_lo(m, 3, int(last >= 4), it))
                                pe.wait_ge(v_copied, at(v_copied, m, 1, it))
                                pe.wait_ge(rt_evac, at(rt_evac, m, 1, it))
                            for j in range(half) if h == 3 else range(half, last + 1):
                                pe.matmul(o_ps, V[:, j, 1:3, :].rearrange("p a d -> p (a d)"),
                                          pT_hi[m % 2][:, j, :, :].rearrange("p h n -> p (h n)"),
                                          start=j == 0, stop=False)
                                ins = pe.matmul(o_ps, V[:, j, 0:2, :].rearrange("p a d -> p (a d)"),
                                                pT_lo[m % 2][:, j, :, :].rearrange("p h n -> p (h n)"),
                                                start=False, stop=j == last)
                                if j == last:
                                    ins.then_inc(pv_done, 1)
                        if h == 3 and real(n - 2, it):
                            m = n - 2
                            if real(n + 1, it):
                                pe.wait_ge(kt_evac, at(kt_evac, n + 1, 1, it))
                            elif real(n - 3, it):
                                pe.wait_ge(add_done, at(add_done, n - 3, 1, it))
                            pe.wait_ge(olo_done, at(olo_done, m, 1, it))
                            if tile(m) == 0:
                                pe.wait_ge(w.lo_done[1], w.at(w.lo_done[1], group(m), 1, it))
                            for i, (q, (op, wp)) in enumerate((q, ps) for q in range(G) for ps in PASSES):
                                ins = pe.matmul(shared[:, 0:D], oT_parts[op][:, q, :], wo[group(m) % 2][wp][:, q, :],
                                                start=i == 0, stop=i == 3 * G - 1)
                            ins.then_inc(op_done, 1)
                spans(pe, step)

            @block.scalar
            def _(a):
                for part in range(2):
                    a.wait_ge(w.loaded[part], count(w.loaded[part], 16))
                    a.activation(w.parts[part][0][0][:, :, :], w.raw[part][:, :, :], ACT.Copy).then_inc(w.hi_done[part], 1)

                def step(n, it):
                    for h in range(G):
                        n2, h2 = two_back(n, h)
                        if real(n2, it):
                            a.wait_ge(t0_done, at(t0_done, n2, h2 + 1, it))
                            if h2 == 0 and real(n2 - 2, it):
                                a.wait_ge(pv_done, at(pv_done, n2 - 2, 1, it))
                            bank, tiles = chunks(n2, h2)[0]
                            a.activation(pT_hi[n2 % 2][:, 0:tiles, h2, :], turned(bank, tiles), ACT.Copy).then_inc(phi0_done, 1)
                            if tile(n2) >= 4:
                                bank, tiles = chunks(n2, h2)[1]
                                a.wait_ge(t1_done, at_late(t1_done, n2, h2, it))
                                a.activation(pT_hi[n2 % 2][:, 4:4 + tiles, h2, :], turned(bank, tiles),
                                             ACT.Copy).then_inc(phi1_done, 1)
                        n1, h1 = (n, h - 1) if h else (n - 1, 3)
                        if real(n1, it):
                            width = (tile(n1) + 1) * P
                            a.wait_ge(max_done, at(max_done, n1, h1 + 1, it))
                            a.activation(prob[h1 % 2][:, 0:width], s_of(h1)[:, 0:width], ACT.Exp,
                                         bias=nmax[:, h1:h1 + 1], scale=1.0,
                                         accum_out=sums[:, n1 % 2, h1:h1 + 1]).then_inc(exp_done, 1)
                        if h == 1 and real(n + 1, it):
                            a.wait_ge(qt_done, at(qt_done, n + 1, 1, it))
                            a.activation(qT[(n + 1) % 2][:, :, :].rearrange("p h n -> p (h n)"),
                                         shared, ACT.Copy, scale=float(HD) ** -0.5).then_inc(qt_evac, 1)
                        if h == 1 and real(n - 2, it):
                            m = n - 2
                            a.wait_ge(norm_done, at(norm_done, m, 1, it))
                            if real(m - 1, it):
                                a.wait_ge(op_done, at(op_done, m - 1, 1, it))
                            a.activation(oT_parts[0][:, :, :], oT[:, :, :], ACT.Copy).then_inc(ohi_done, 1)
                        if h == 3:
                            for part, t, freed in ((0, 2, proj_done), (1, 5, op_done)):
                                g = split_group(n, t, it)
                                if g is not None:
                                    if g >= 2 or it is not None:
                                        a.wait_ge(freed, at(freed, 8 * g - 7, 1, it))
                                    a.wait_ge(w.loaded[part], w.at(w.loaded[part], g, 16, it))
                                    a.activation(w.parts[part][g % 2][0][:, :, :], w.raw[part][:, :, :],
                                                 ACT.Copy).then_inc(w.hi_done[part], 1)
                        if h == 2 and real(n + 1, it):
                            m = n + 1
                            a.wait_ge(kt_done, at(kt_done, m, 1, it))
                            a.activation(kT[group(m) % 2][:, :, tile(m) * P:(tile(m) + 1) * P],
                                         shared[:, 0:2 * P].rearrange("p (a n) -> p a n", a=2), ACT.Copy).then_inc(kt_evac, 1)
                        if h == 2 and real(n - 1, it):
                            a.wait_ge(rt_done, at(rt_done, n - 1, 1, it))
                            if real(n - 2, it):
                                a.wait_ge(norm_done, at(norm_done, n - 2, 1, it))
                            a.activation(rec_rows[:, :], rec_ps, ACT.Copy).then_inc(rt_evac, 1)
                spans(a, step)

            @block.vector
            def _(v):
                v.wait_ge(w.rope_loaded, count(w.rope_loaded, 16))
                for i in range(2):
                    v.memset(vv[i][:, :, 0, :].bitcast(F32), 0.0)

                def step(n, it):
                    for h in range(G):
                        n2, h2 = two_back(n, h)
                        if real(n2, it):
                            if h2 == 0 and real(n2 - 2, it):
                                v.wait_ge(pv_done, at(pv_done, n2 - 2, 1, it))
                            bank, tiles = chunks(n2, h2)[0]
                            v.wait_ge(phi0_done, at(phi0_done, n2, h2 + 1, it))
                            v.tensor_tensor(pT_lo[n2 % 2][:, 0:tiles, h2, :], turned(bank, tiles),
                                            pT_hi[n2 % 2][:, 0:tiles, h2, :].bitcast(F32),
                                            ALU.subtract).then_inc(plo_done, 1)
                            if tile(n2) >= 4:
                                bank, tiles = chunks(n2, h2)[1]
                                v.wait_ge(phi1_done, at_late(phi1_done, n2, h2, it))
                                v.tensor_tensor(pT_lo[n2 % 2][:, 4:4 + tiles, h2, :], turned(bank, tiles),
                                                pT_hi[n2 % 2][:, 4:4 + tiles, h2, :].bitcast(F32),
                                                ALU.subtract).then_inc(plo_done, 1)
                        if real(n, it):
                            v.wait_ge(s_done, at(s_done, n, h + 1, it))
                            v.tensor_reduce(nmax[:, h:h + 1], s_of(h)[:, 0:(tile(n) + 1) * P],
                                            AX.X, ALU.max, negate=True).then_inc(max_done, 1)
                        if h == 0 and real(n + 2, it):
                            m = n + 2
                            t = tile(m)
                            v.wait_ge(proj_done, at(proj_done, m, 1, it))
                            if real(m - 1, it):
                                v.wait_ge(hi_done, at(hi_done, m - 1, 2, it))
                            qk_ps = shared[:, 0:5 * HD].rearrange("p (h d) -> p h d", h=5)
                            v.tensor_tensor(ra[:, :, :], qk_ps, ax(rope[:, 0, t, :], 5), ALU.mult)
                            v.tensor_tensor(rb[:, :, 0:HD // 2], qk_ps[:, :, HD // 2:HD],
                                            ax(rope[:, 1, t, 0:HD // 2], 5), ALU.mult)
                            v.tensor_tensor(rb[:, :, HD // 2:HD], qk_ps[:, :, 0:HD // 2],
                                            ax(rope[:, 1, t, HD // 2:HD], 5), ALU.mult).then_inc(rope_done, 1)
                            V = vv[group(m) % 2]
                            v_hi, v_lo = V[:, t, 1, :], V[:, t, 2, :]
                            v.tensor_copy(v_hi, shared[:, GW - HD:GW]).then_inc(v_hi_done, 1)
                            v.wait_ge(v_hi_done, at(v_hi_done, m, 1, it))
                            v.tensor_tensor(v_lo, shared[:, GW - HD:GW], v_hi.bitcast(F32),
                                            ALU.subtract).then_inc(v_copied, 1)
                        if h == 1 and real(n - 1, it):
                            m = n - 1
                            v.wait_ge(exp_done, at(exp_done, m, 4, it))
                            v.reciprocal(rec[:, m % 2, :], sums[:, m % 2, :]).then_inc(rec_done, 1)
                        if h == 0 and real(n - 2, it):
                            m = n - 2
                            v.wait_ge(rt_evac, at(rt_evac, m, 1, it))
                            v.wait_ge(pv_done, at(pv_done, m, 1, it))
                            if real(m - 1, it):
                                v.wait_ge(olo_done, at(olo_done, m - 1, 1, it))
                            v.tensor_tensor(oT[:, :, :].rearrange("p h n -> p (h n)"), o_ps, rec_rows[:, :],
                                            ALU.mult).then_inc(norm_done, 1)
                        if h == 3 and real(n - 2, it):
                            m = n - 2
                            v.wait_ge(op_done, at(op_done, m, 1, it))
                            v.tensor_tensor(acc[:, tile(m), :], acc[:, tile(m), :], shared[:, 0:D], ALU.add).then_inc(add_done, 1)
                spans(v, step)

            @block.sync
            def _(sp):
                with sp.Fori(0, HKV - 1, 1) as it:
                    for part in range(2):
                        sp.wait_ge(w.lo_done[part], count(w.lo_done[part], 1, (it, 1)))
                        w.load(sp, part, bass.ds(it * P + P, P))

            @block.gpsimd
            def _(g):
                for part in range(2):
                    hi, lo = w.parts[part][0]
                    g.wait_ge(w.hi_done[part], count(w.hi_done[part], 1))
                    g.tensor_tensor(lo[:, :, :], w.raw[part][:, :, :], hi[:, :, :].bitcast(F32),
                                    ALU.subtract).then_inc(w.lo_done[part], 1)

                def step(n, it):
                    if real(n - 2, it):
                        m = n - 2
                        g.wait_ge(ohi_done, at(ohi_done, m, 1, it))
                        g.tensor_tensor(oT_parts[1][:, :, :], oT[:, :, :], oT_parts[0][:, :, :].bitcast(F32),
                                        ALU.subtract).then_inc(olo_done, 1)
                    if real(n + 2, it):
                        m = n + 2
                        parts = qk[m % 2]
                        g.wait_ge(rope_done, at(rope_done, m, 1, it))
                        if real(m - 2, it):
                            g.wait_ge(kt_done, at(kt_done, m - 2, 1, it))
                        if real(m - 1, it):
                            g.wait_ge(split_done, at(split_done, m - 1, 1, it))
                        g.tensor_tensor(rs[:, :, :], ra[:, :, :], rb[:, :, :], ALU.add).then_inc(sum_done, 1)
                        g.tensor_tensor(parts[:, 0:4, 0:HD], ra[:, 0:4, :], rb[:, 0:4, :], ALU.add).then_inc(hi_done, 1)
                        g.tensor_tensor(parts[:, 4, :].rearrange("p (a d) -> p a d", a=2),
                                        ax(ra[:, 4, :], 2), ax(rb[:, 4, :], 2), ALU.add).then_inc(hi_done, 1)
                        g.wait_ge(sum_done, at(sum_done, m, 1, it))
                        g.wait_ge(hi_done, at(hi_done, m, 2, it))
                        g.tensor_tensor(parts[:, 0:4, HD:P], rs[:, 0:4, :], parts[:, 0:4, 0:HD].bitcast(F32),
                                        ALU.subtract)
                        g.tensor_tensor(parts[:, 5, :].rearrange("p (a d) -> p a d", a=2),
                                        ax(rs[:, 4, :], 2),
                                        parts[:, 4, :].rearrange("p (a d) -> p a d", a=2).bitcast(F32),
                                        ALU.subtract).then_inc(split_done, 1)
                    for part, t in ((0, 2), (1, 5)):
                        grp = split_group(n, t, it)
                        if grp is not None:
                            hi, lo = w.parts[part][grp % 2]
                            g.wait_ge(w.hi_done[part], w.at(w.hi_done[part], grp, 1, it))
                            g.tensor_tensor(lo[:, :, :], w.raw[part][:, :, :], hi[:, :, :].bitcast(F32),
                                            ALU.subtract).then_inc(w.lo_done[part], 1)
                spans(g, step)

        counts = {s: k * STEPS for s, k in per_step.items()}
        counts.update({t1_done: 16 * HKV, phi1_done: 16 * HKV, plo_done: 4 * STEPS + 16 * HKV})
        counts.update({sem: 16 * HKV for sem in w.loaded})
        counts[w.rope_loaded] = 16
        counts.update({sem: HKV for sem in w.hi_done + w.lo_done})
        c.done(counts)



def router(c, hT, wg, gates):
    nc, count, own = c.nc, c.count, c.own
    with ExitStack() as ctx:
        ph = c.phase
        c.phase += 1
        sb = lambda name, shape, dt=F32: c.sb(f"{name}{ph}", shape, dt, ctx)
        logits = sb("logits", [P, NT, NE])
        top = sb("top", [P, NT, 8])
        idx = sb("top_idx", [P, NT, 8], U32)
        idxf = sb("top_idxf", [P, NT, 8])
        ex = sb("top_exp", [P, NT, TOPK])
        den = sb("top_den", [P, NT])
        eq = sb("top_eq", [P, TOPK, NT, NE])
        wsum = sb("gate_rows", [P, NT, NE])
        logits_done, ready, exps = (c.sem(x) for x in ("rt_logits", "rt_shifted", "rt_exp"))
        dve = c.sem("dve_own")
        iota = c.consts[:, 0:NE]
        with nc.Block() as block:
            @block.tensor
            def _(pe):
                for t in range(NT):
                    for k in range(DK):
                        ins = pe.matmul(c.psum[:, 0, t * NE:(t + 1) * NE], hT[:, k, t * P:(t + 1) * P],
                                        wg[:, k, :], start=k == 0, stop=k == DK - 1)
                ins.then_inc(logits_done, 1)

            @block.scalar
            def _(a):
                a.wait_ge(ready, count(ready, 1))
                a.activation(ex[:, :, :], ex[:, :, :], ACT.Exp).then_inc(exps, 1)

            @block.vector
            def _(v):
                v.wait_ge(logits_done, count(logits_done, 1))
                v.tensor_copy(logits[:, :, :].rearrange("p t e -> p (t e)"), c.psum[:, 0, 0:NT * NE]).then_inc(dve, 1)
                v.wait_ge(dve, own(dve))
                for t in range(NT):
                    ins = v.max(top[:, t, :], logits[:, t, :])
                ins.then_inc(dve, 1)
                v.wait_ge(dve, own(dve))
                for t in range(NT):
                    ins = v.max_index(idx[:, t, :], top[:, t, :], logits[:, t, :])
                ins.then_inc(dve, 1)
                v.wait_ge(dve, own(dve))
                v.tensor_copy(idxf[:, :, :], idx[:, :, :])
                v.tensor_tensor(ex[:, :, :], top[:, :, 0:TOPK], bx(top[:, :, 0], TOPK), ALU.subtract).then_inc(ready, 1)
                v.wait_ge(exps, count(exps, 1))
                v.tensor_reduce(den[:, :], ex[:, :, :], AX.X, ALU.add).then_inc(dve, 1)
                v.wait_ge(dve, own(dve))
                v.reciprocal(den[:, :], den[:, :]).then_inc(dve, 1)
                v.wait_ge(dve, own(dve))
                v.tensor_tensor(ex[:, :, :], ex[:, :, :], bx(den[:, :], TOPK), ALU.mult).then_inc(dve, 1)
                v.wait_ge(dve, own(dve))
                for k in range(TOPK):
                    ins = v.tensor_tensor(eq[:, k, :, :], ax(iota, NT), bx(idxf[:, :, k], NE), ALU.is_equal)
                ins.then_inc(dve, 1)
                v.wait_ge(dve, own(dve))
                for k in range(TOPK):
                    ins = v.tensor_tensor(eq[:, k, :, :], eq[:, k, :, :], bx(ex[:, :, k], NE), ALU.mult)
                ins.then_inc(dve, 1)
                v.wait_ge(dve, own(dve))
                for k in (0, 2):
                    ins = v.tensor_tensor(eq[:, k, :, :], eq[:, k, :, :], eq[:, k + 1, :, :], ALU.add)
                ins.then_inc(dve, 1)
                v.wait_ge(dve, own(dve))
                v.tensor_tensor(gates[:, :, :].rearrange("p e t -> p t e"), eq[:, 0, :, :], eq[:, 2, :, :], ALU.add)
        c.done({logits_done: 1, ready: 1, exps: 1})



class ExpertWeights:

    def __init__(self, c, ctx, dram):
        self.raw = [c.sb(f"w_raw{c.phase}_{i}", [P, 3, DK, HH], F32, ctx) for i in range(2)]
        self.loaded = [c.sem(f"mx_load{i}") for i in range(2)]
        self.dram = dram.rearrange("e p n -> (e p) n")

    def load(self, sp, slot, rows):
        sp.dma_start(self.raw[slot][:, :, :, :].rearrange("p a k n -> p (a k n)"), self.dram[rows, :])\
            .then_inc(self.loaded[slot], 16)

    def load_first(self, sp):
        for e in range(2):
            self.load(sp, e, slice(e * P, (e + 1) * P))


def experts(c, h_hi, h_lo, gates, weights, acc):
    nc, count, own = c.nc, c.count, c.own
    banks = c.psum
    names = ["mx_whi", "mx_wlo", "mx_a", "mx_tanh", "mx_t1", "mx_s", "mx_hi", "mx_lo", "mx_y", "mx_acc"]
    whi_done, wlo_done, a_done, tanh_done, t1_done, s_done, hi_done, lo_done, y_done, acc_done = (
        c.sem(x) for x in names)
    raw, loaded = weights.raw, weights.loaded
    with ExitStack() as ctx:
        ph = c.phase
        c.phase += 1
        sb = lambda name, shape, dt=F32: c.sb(f"{name}{ph}", shape, dt, ctx)
        whi = [sb(f"w_hi{i}", [P, 3, DK, HH], F32R) for i in range(2)]
        wlo = [sb(f"w_lo{i}", [P, 3, DK, HH], F32R) for i in range(2)]
        th = [sb(f"tanh{i}", [P, 512]) for i in range(2)]
        s1 = [sb(f"silu{i}", [P, 512]) for i in range(2)]
        s2 = [sb(f"hid{i}", [P, 512]) for i in range(2)]
        ahi = [sb(f"hid_hi{i}", [P, 2, 512], F32R) for i in range(2)]
        alo = [sb(f"hid_lo{i}", [P, 2, 512], F32R) for i in range(2)]
        gflat = gates[:, :, :].rearrange("p e t -> p (e t)")
        NH2 = 2 * NE

        def lp(it, k):
            return None if it is None else (it, k)

        def ok(q, it):
            return it is not None or 0 <= q < NH2

        def spans(eng, program, first):
            turns = NE // 2 - 2
            for q in range(-1, first):
                program(q, None)
            with eng.Fori(0, turns, 1) as it:
                for q in range(first, first + 4):
                    program(q, it)
            for q in range(first + 4 * turns, NH2):
                program(q, None)

        PASSES = ((0, 0), (0, 1), (1, 0))
        with nc.Block() as block:
            @block.sync
            def _(sp):
                with sp.Fori(0, NE // 2 - 1, 1) as it:
                    for j in range(2):
                        sp.wait_ge(whi_done, count(whi_done, j + 1, (it, 2)))
                        sp.wait_ge(wlo_done, count(wlo_done, j + 1, (it, 2)))
                        weights.load(sp, j, bass.ds(it * (2 * P) + (j + 2) * P, P))

            @block.tensor
            def _(pe):
                def program(q, it):
                    r = q + 1
                    if ok(r, it):
                        e, s = r // 2, r % 2
                        if s == 0:
                            pe.wait_ge(wlo_done, count(wlo_done, e + 1, lp(it, 2)))
                            pe.wait_ge(whi_done, count(whi_done, e + 1, lp(it, 2)))
                        W, H = (whi[e % 2], wlo[e % 2]), (h_hi, h_lo)
                        for m in range(2):
                            unit = 2 * r + m
                            if it is not None or unit >= 2:
                                pe.wait_ge(s_done, count(s_done, unit - 1, lp(it, 8)))
                            for mat in range(2):
                                for n, (k, (wp, hp)) in enumerate((k, ps) for k in range(DK) for ps in PASSES):
                                    ins = pe.matmul(banks[:, 2 * (unit % 2) + mat, :], W[wp][:, mat, k, m * P:(m + 1) * P],
                                                    H[hp][:, k, s * 512:(s + 1) * 512], start=n == 0, stop=n == 5)
                            ins.then_inc(a_done, 1)
                    if ok(q, it):
                        e, s = q // 2, q % 2
                        W, A = (whi[e % 2], wlo[e % 2]), (ahi[s], alo[s])
                        pe.wait_ge(hi_done, count(hi_done, 2 * q + 2, lp(it, 8)))
                        pe.wait_ge(lo_done, count(lo_done, 2 * q + 2, lp(it, 8)))
                        for j in range(4):
                            if j % 2 == 0 and (it is not None or q >= 2):
                                pe.wait_ge(acc_done, count(acc_done, 2 * (q - 2) + j // 2 + 1, lp(it, 8)))
                            for n, (k, (ap, wp)) in enumerate((k, ps) for k in range(DK) for ps in PASSES):
                                ins = pe.matmul(banks[:, 4 + 2 * s + j // 2, (j % 2) * D:(j % 2 + 1) * D],
                                                A[ap][:, k, j * P:(j + 1) * P], W[wp][:, 2, k, :],
                                                start=n == 0, stop=n == 5)
                            if j % 2:
                                ins.then_inc(y_done, 1)
                spans(pe, program, 3)

            @block.scalar
            def _(a):
                def split(e, it):
                    a.wait_ge(loaded[e % 2], count(loaded[e % 2], 16 * (e // 2 + 1), lp(it, 16)))
                    if it is not None or e >= 2:
                        a.wait_ge(y_done, count(y_done, 4 * (e - 1), lp(it, 8)))
                    a.activation(whi[e % 2][:, :, :, :], raw[e % 2][:, :, :, :], ACT.Copy).then_inc(whi_done, 1)

                def program(q, it):
                    if q < 0:
                        return split(0, None)
                    for m in range(2):
                        unit = 2 * q + m
                        a.wait_ge(a_done, count(a_done, unit + 1, lp(it, 8)))
                        if it is not None or unit >= 2:
                            a.wait_ge(t1_done, count(t1_done, unit - 1, lp(it, 8)))
                        a.activation(th[m][:, :], banks[:, 2 * m, :], ACT.Tanh, scale=0.5).then_inc(tanh_done, 1)
                        a.wait_ge(s_done, count(s_done, unit + 1, lp(it, 8)))
                        if it is not None or q >= 2:
                            a.wait_ge(y_done, count(y_done, 2 * (q - 1), lp(it, 8)))
                        a.activation(ahi[q % 2][:, m, :], s2[m][:, :], ACT.Copy).then_inc(hi_done, 1)
                    if q % 2 == 0 and (it is not None or q // 2 + 1 < NE):
                        split(q // 2 + 1, it)
                spans(a, program, 3)

            @block.vector
            def _(v):
                def program(q, it):
                    if q >= 0:
                        for m in range(2):
                            unit = 2 * q + m
                            v.wait_ge(tanh_done, count(tanh_done, unit + 1, lp(it, 8)))
                            if it is not None or unit >= 2:
                                v.wait_ge(s_done, count(s_done, unit - 1, lp(it, 8)))
                            v.scalar_tensor_tensor(out=s1[m][:, :], in0=th[m][:, :], scalar=1.0,
                                                   in1=banks[:, 2 * m, :], op0=ALU.add, op1=ALU.mult).then_inc(t1_done, 1)
                            v.wait_ge(t1_done, count(t1_done, unit + 1, lp(it, 8)))
                            if it is not None or unit >= 2:
                                v.wait_ge(lo_done, count(lo_done, unit - 1, lp(it, 8)))
                                v.wait_ge(hi_done, count(hi_done, unit - 1, lp(it, 8)))
                            v.scalar_tensor_tensor(out=s2[m][:, :], in0=s1[m][:, :], scalar=0.5,
                                                   in1=banks[:, 2 * m + 1, :], op0=ALU.mult, op1=ALU.mult).then_inc(s_done, 1)
                            v.wait_ge(hi_done, count(hi_done, unit + 1, lp(it, 8)))
                            if m == 0 and (it is not None or q >= 2):
                                v.wait_ge(y_done, count(y_done, 2 * (q - 1), lp(it, 8)))
                            v.tensor_tensor(alo[q % 2][:, m, :], s2[m][:, :],
                                            ahi[q % 2][:, m, :].bitcast(F32), ALU.subtract).then_inc(lo_done, 1)
                    p = q - 1
                    if ok(p, it):
                        add(p, it)

                def add(p, it):
                    e, s = p // 2, p % 2
                    for j in range(4):
                        t = 4 * s + j
                        if j % 2 == 0:
                            v.wait_ge(y_done, count(y_done, 2 * p + j // 2 + 1, lp(it, 8)))
                        if j == 0 and (it is not None or p >= 2):
                            v.wait_ge(acc_done, count(acc_done, 2 * (p - 1), lp(it, 8)))
                        gate = (gflat[:, e * NT + t:e * NT + t + 1] if it is None
                                else gflat[:, bass.ds(it * (2 * NT) + (e * NT + t), 1)])
                        ins = v.scalar_tensor_tensor(out=acc[:, t, :], scalar=gate, in1=acc[:, t, :],
                                                     in0=banks[:, 4 + 2 * s + j // 2, (j % 2) * D:(j % 2 + 1) * D],
                                                     op0=ALU.mult, op1=ALU.add)
                        if j % 2:
                            ins.then_inc(acc_done, 1)
                spans(v, program, 3)
                add(NH2 - 1, None)

            @block.gpsimd
            def _(g):
                def split(e, it):
                    g.wait_ge(whi_done, count(whi_done, e + 1, lp(it, 2)))
                    if it is not None or e >= 2:
                        g.wait_ge(y_done, count(y_done, 4 * (e - 1), lp(it, 8)))
                    g.tensor_tensor(wlo[e % 2][:, :, :, :], raw[e % 2][:, :, :, :],
                                    whi[e % 2][:, :, :, :].bitcast(F32), ALU.subtract).then_inc(wlo_done, 1)
                split(0, None)
                split(1, None)
                with g.Fori(0, NE // 2 - 1, 1) as it:
                    split(2, it)
                    split(3, it)
        c.done({loaded[0]: 8 * NE, loaded[1]: 8 * NE, whi_done: NE, wlo_done: NE, a_done: 4 * NE, tanh_done: 4 * NE, t1_done: 4 * NE,
                s_done: 4 * NE, hi_done: 4 * NE, lo_done: 4 * NE, y_done: 4 * NE, acc_done: 4 * NE})



class MambaMemory:
    def __init__(self, c, ctx):
        sb = lambda name, shape, dt=F32: c.sb("mb_" + name, shape, dt, ctx)
        self.hT = sb("hT", [P, DK, L])
        self.w_in = sb("w_in", [P, DK, 2 * INNER + 2 * DST + NH])
        self.w_out = sb("w_out", [P, NZ, D])
        self.cols = sb("cols", [P, 48])
        self.rows = sb("rows", [P, 3 * NH + D])
        self.scan = sb("scan", [P, 5 * P + CH])
        self.zT = sb("zT", [P, NZ, L])
        self.xT = sb("xT", [P, NZ, L])
        self.bcT = sb("bcT", [P, 2, L])
        self.btok = sb("btok", [P, NT, DST])
        self.xd = sb("xd", [P, NT, INNER])
        self.dA = sb("dA", [P, NT * NH])
        self.rev = sb("rev", [P, NT * NH])
        self.tot = sb("tot", [P, 2, NT * NH])
        self.head = sb("head", [CH, 2, NT * NH])
        self.b_z, self.b_x = self.cols[:, 0:4], self.cols[:, 4:10]
        self.conv_w = self.cols[:, 10:34].rearrange("p (m j) -> p m j", j=TAPS)
        self.conv_b = self.cols[:, 34:40]
        self.d_col, self.norm_w = self.cols[:, 40:44], self.cols[:, 44:48]
        self.later = self.scan[:, 0:P]
        self.upto = self.scan[:, P:2 * P].rearrange("p (c l) -> p c l", c=2)
        self.whole = self.scan[:, 2 * P:4 * P].rearrange("p (c n) -> p c n", c=2)
        self.within = self.scan[:, 4 * P:4 * P + CH]
        self.ones = self.scan[:, 5 * P:5 * P + 1]


def mamba_front(c, m):
    nc, count, own = c.nc, c.count, c.own
    banks = c.psum
    with ExitStack() as ctx:
        sb = lambda name, shape, dt=F32: c.sb("mf_" + name, shape, dt, ctx)
        raw = [sb(f"raw{i}", [P, L + 4]) for i in range(2)]
        th = [sb(f"tanh{i}", [P, L]) for i in range(2)]
        pre = [sb(f"pre{i}", [P, L]) for i in range(2)]
        dt = sb("dt", [P, NT, NH])
        arow = sb("arow", [P, NH])
        dtb = sb("dtb", [P, NH])
        half = sb("half", [P, 10])
        names = ["mf_dt", "mf_dtb", "mf_sp", "mf_dtok", "mf_sum", "mf_dec", "mf_pj", "mf_pre", "mf_half", "mf_conv",
                 "mf_th", "mf_out", "mf_tr", "mf_trev", "mf_arow", "mf_acc", "mf_bev"]
        (dt_mm, dt_in, softplus, dt_ok, sum_mm, decays, proj, pre_done, halved, conv_done, tanh_done, out_done,
         tr_done, tr_evac, arow_done, taps_done, b_evac) = (c.sem(x) for x in names)
        dve, act, pool = c.sem("dve_own"), c.sem("act_own"), c.sem("pool_own")
        z0, x0, dt0 = 0, INNER, INNER + CONVD
        NF = NZ + NX

        with nc.Block() as block:
            @block.tensor
            def _(pe):
                for t in range(NT):
                    for k in range(DK):
                        ins = pe.matmul(banks[:, 7, t * NH:(t + 1) * NH], m.hT[:, k, t * P:(t + 1) * P],
                                        m.w_in[:, k, dt0:dt0 + NH], start=k == 0, stop=k == DK - 1)
                ins.then_inc(dt_mm, 1)

                def project(f):
                    if f >= 2:
                        pe.wait_ge(pre_done, count(pre_done, 2 * (f - 1)))
                    for s in range(2):
                        for k in range(DK):
                            ins = pe.matmul(banks[:, 2 * (f % 2) + s, :], m.w_in[:, k, f * P:(f + 1) * P],
                                            m.hT[:, k, s * 512:(s + 1) * 512], start=k == 0, stop=k == DK - 1)
                        ins.then_inc(proj, 1)

                def turn(f):
                    r = f - NZ
                    pe.wait_ge(out_done, count(out_done, f + 1))
                    src = m.xT[:, r, :] if r < NZ else m.bcT[:, 0, :]
                    for s in range(2):
                        if r:
                            pe.wait_ge(tr_evac, count(tr_evac, 2 * (r - 1) + s + 1))
                        for j in range(4):
                            ins = pe.transpose(banks[:, 4 + s, j * P:(j + 1) * P],
                                               src[:, (4 * s + j) * P:(4 * s + j + 1) * P], c.ident[:, :])
                        ins.then_inc(tr_done, 1)

                for f in range(NF):
                    project(f)
                    if f == 1:
                        pe.wait_ge(dt_ok, count(dt_ok, 1))
                        for n in range(5):
                            lhs, rows = ((m.upto[:, 0, :], CH), (m.upto[:, 1, :], CH), (m.later, P),
                                         (m.whole[:, 0, :], P), (m.whole[:, 1, :], P))[n]
                            if n:
                                pe.wait_ge(decays, count(decays, n))
                            pe.matmul(banks[0:rows, 6, :], lhs, m.dA[:, :], start=True, stop=True).then_inc(sum_mm, 1)
                    if f >= NZ + 2 and f - 2 < NF - 1:
                        turn(f - 2)
                turn(NF - 2)

            @block.scalar
            def _(a):
                a.activation(arow[:, :], m.rows[:, 2 * NH:3 * NH], ACT.Exp).then_inc(arow_done, 1)
                a.wait_ge(dt_in, count(dt_in, 1))
                a.activation(dt[:, :, :], dt[:, :, :], ACT.Exp).then_inc(act, 1)
                a.wait_ge(act, own(act))
                a.activation(dt[:, :, :], dt[:, :, :], ACT.Ln, bias=1.0).then_inc(softplus, 1)
                a.wait_ge(halved, count(halved, 1))

                def pre_of(f):
                    for s in range(2):
                        a.wait_ge(proj, count(proj, 2 * f + s + 1))
                        if f >= 2 and s == 0:
                            a.wait_ge(out_done, count(out_done, f - 1))
                        if f < NZ:
                            ins = a.activation(pre[f % 2][:, s * 512:(s + 1) * 512], banks[:, 2 * (f % 2) + s, :],
                                               ACT.Identity, bias=half[:, f:f + 1], scale=0.5)
                        else:
                            ins = a.activation(raw[f % 2][:, 3 + s * 512:3 + (s + 1) * 512],
                                               banks[:, 2 * (f % 2) + s, :], ACT.Identity,
                                               bias=m.b_x[:, f - NZ:f - NZ + 1], scale=1.0)
                        ins.then_inc(pre_done, 1)

                def tanh_of(f):
                    if f < NZ:
                        a.wait_ge(pre_done, count(pre_done, 2 * f + 2))
                    else:
                        a.wait_ge(conv_done, count(conv_done, f - NZ + 1))
                    a.activation(th[f % 2][:, :], pre[f % 2][:, :], ACT.Tanh).then_inc(tanh_done, 1)

                pre_of(0)
                for f in range(NF):
                    if f == 1:
                        for n, dst in enumerate((m.head[:, 0, :], m.head[:, 1, :], m.rev[:, :], m.tot[:, 0, :],
                                                 m.tot[:, 1, :])):
                            a.wait_ge(sum_mm, count(sum_mm, n + 1))
                            a.activation(dst, banks[0:dst.shape[0], 6, :], ACT.Exp).then_inc(decays, 1)
                    if f + 1 < NF and f + 1 < NZ:
                        tanh_of(f)
                        pre_of(f + 1)
                    else:
                        if f + 1 < NF:
                            pre_of(f + 1)
                        tanh_of(f)
                for s in range(2):
                    a.wait_ge(tr_done, count(tr_done, 2 * NZ + s + 1))
                    a.activation(m.btok[:, 4 * s:4 * s + 4, :].rearrange("p t n -> p (t n)"),
                                  banks[:, 4 + s, :], ACT.Copy).then_inc(b_evac, 1)

            @block.gpsimd
            def _(g):
                g.tensor_tensor(c.x[:, :, :], c.x[:, :, :], ax(m.rows[:, 3 * NH:3 * NH + D], NT), ALU.add)
                for i in range(2):
                    g.memset(raw[i][:, 0:3], 0.0)
                for j in range(NZ):
                    g.tensor_scalar(m.w_out[:, j, :], m.w_out[:, j, :], m.norm_w[:, j:j + 1], None, ALU.mult)
                g.memset(half[:, 9:10], 0.0).then_inc(pool, 1)
                g.wait_ge(pool, own(pool))
                g.nop().then_inc(taps_done, 1)

            @block.vector
            def _(v):
                v.tensor_scalar(half[:, 0:NZ], m.b_z, 0.5, None, ALU.mult)
                v.tensor_scalar(m.cols[:, 10:40], m.cols[:, 10:40], 0.5, None, ALU.mult).then_inc(halved, 1)
                v.tensor_tensor(dtb[:, :], m.rows[:, 0:NH], m.rows[:, NH:2 * NH], ALU.add).then_inc(dve, 1)
                v.wait_ge(dve, own(dve))
                v.wait_ge(dt_mm, count(dt_mm, 1))
                v.tensor_tensor(dt[:, :, :], banks[:, 7, :].rearrange("p (t h) -> p t h", t=NT),
                                ax(dtb[:, :], NT), ALU.add).then_inc(dve, 1)
                v.wait_ge(dve, own(dve))
                v.tensor_scalar(dt[:, :, :], dt[:, :, :], 20.0, None, ALU.min).then_inc(dt_in, 1)
                v.wait_ge(softplus, count(softplus, 1))
                v.wait_ge(arow_done, count(arow_done, 1))
                v.tensor_scalar(dt[:, :, :], dt[:, :, :], 0.001, 0.1, ALU.max, ALU.min).then_inc(dve, 1)
                v.wait_ge(dve, own(dve))
                v.tensor_scalar(arow[:, :], arow[:, :], -1.0, None, ALU.mult).then_inc(dve, 1)
                v.wait_ge(dve, own(dve))
                v.tensor_tensor(m.dA[:, :].rearrange("p (t h) -> p t h", t=NT), dt[:, :, :],
                                ax(arow[:, :], NT), ALU.mult).then_inc(dt_ok, 1)
                v.wait_ge(taps_done, count(taps_done, 1))

                def gate_of(f):
                    dst = m.zT[:, f, :] if f < NZ else m.xT[:, f - NZ, :] if f < 2 * NZ else m.bcT[:, f - 2 * NZ, :]
                    v.wait_ge(tanh_done, count(tanh_done, f + 1))
                    v.scalar_tensor_tensor(out=dst, in0=th[f % 2][:, :], scalar=1.0,
                                           in1=pre[f % 2][:, :], op0=ALU.add, op1=ALU.mult).then_inc(out_done, 1)

                def evac_of(f):
                    r = f - NZ
                    for s in range(2):
                        v.wait_ge(tr_done, count(tr_done, 2 * r + s + 1))
                        out = m.xd[:, 4 * s:4 * s + 4, r * P:(r + 1) * P].rearrange("p t (h q) -> p t h q", q=HP)
                        v.tensor_tensor(out, banks[:, 4 + s, :].rearrange("p (t h q) -> p t h q", t=4, q=HP),
                                        bx(dt[:, 4 * s:4 * s + 4, r * 16:(r + 1) * 16], HP), ALU.mult).then_inc(tr_evac, 1)

                for f in range(NF):
                    if f >= NZ:
                        r = f - NZ
                        v.wait_ge(pre_done, count(pre_done, 2 * f + 2))
                        src, dst = raw[f % 2], pre[f % 2][:, :]
                        if r == 0:
                            v.wait_ge(out_done, count(out_done, f))
                        v.tensor_scalar(dst, src[:, 3:3 + L], m.conv_w[:, r, 3:4], m.conv_b[:, r:r + 1],
                                        ALU.mult, ALU.add).then_inc(dve, 1)
                        v.wait_ge(dve, own(dve))
                        for j in range(3):
                            ins = v.scalar_tensor_tensor(out=dst, in0=src[:, j:j + L], scalar=m.conv_w[:, r, j:j + 1],
                                                         in1=dst, op0=ALU.mult, op1=ALU.add)
                            if j < 2:
                                ins.then_inc(dve, 1)
                                v.wait_ge(dve, own(dve))
                        ins.then_inc(conv_done, 1)
                    gate_of(f)
                    if f >= NZ + 2 and f - 2 < 2 * NZ:
                        evac_of(f - 2)
        c.done({dt_mm: 1, dt_in: 1, softplus: 1, dt_ok: 1, sum_mm: 5, decays: 5, proj: 2 * NF, pre_done: 2 * NF,
                halved: 1, conv_done: NX, tanh_done: NF, out_done: NF, tr_done: 2 * NZ + 2, tr_evac: 2 * NZ, b_evac: 2,
                arow_done: 1, taps_done: 1})


def mamba_scan(c, m):
    nc, count, own = c.nc, c.count, c.own
    banks = c.psum
    diag = banks[0:CH, 2:4, :].rearrange("p b n -> p (b n)")
    shared = banks[:, 7, :]
    names = ["ms_stage", "ms_xdb", "ms_xdr", "ms_g", "ms_gm", "ms_rb", "ms_seg", "ms_l", "ms_m", "ms_yd", "ms_off",
             "ms_st", "ms_tmp", "ms_upd", "ms_y1", "ms_y", "ms_t", "ms_yt", "ms_gz", "ms_sq", "ms_out", "ms_var",
             "ms_pow", "ms_x", "ms_init", "ms_split"]
    (stage_done, xdb_done, xdr_done, g_done, gm_done, rb_done, seg_done, l_done, m_done, yd_done, off_done, st_done,
     tmp_done, upd_done, y1_done, y_done, t_done, yt_done, gz_done, sq_done, out_done, var_done, pow_done, x_done,
     init_done, split_done) = (c.sem(x) for x in names)
    pool = c.sem("pool_own")
    per = {s: 1 for s in (stage_done, xdb_done, xdr_done, g_done, gm_done, y1_done, y_done, t_done, yt_done, gz_done,
                          sq_done, out_done, var_done, pow_done, x_done)}
    per.update({s: 8 for s in (rb_done, seg_done, l_done, m_done, yd_done)})
    per.update({s: 2 for s in (off_done, st_done, tmp_done, upd_done)})
    NG = NH // 8
    with ExitStack() as ctx:
        sb = lambda name, shape, dt=F32: c.sb("ms_" + name, shape, dt, ctx)
        bcs = [sb(f"bc{i}", [P, 2, P]) for i in range(2)]
        bts = [sb(f"bt{i}", [P, DST]) for i in range(2)]
        xdb = [sb(f"xdb{i}", [P, NH, 2, HP]) for i in range(2)]
        xdr = [sb(f"xdr{i}", [P, INNER]) for i in range(2)]
        gm = [sb(f"gm{i}", [P, CH]) for i in range(2)]
        rbuf = [sb(f"rb{i}", [P, 2, 8, CH], F32R) for i in range(2)]
        dA_hi = sb("dA_hi", [P, NT * NH], F32R)
        dA_lo = sb("dA_lo", [P, NT * NH])
        later = sb("later", [P, P], F32R)
        lbuf = [sb(f"l{i}", [P, 8, CH]) for i in range(2)]
        mbuf = [sb(f"m{i}", [P, 8, CH]) for i in range(2)]
        state = [sb(f"state{i}", [P, INNER]) for i in range(2)]
        tmp = sb("tmp", [P, INNER])
        ysb = sb("y", [CH, 2, INNER])
        yT = sb("yT", [P, NZ, P])
        gz = sb("gz", [P, NZ, P])
        sq = sb("sq", [P, NZ, P])
        var = sb("var", [P, 4])
        x_flat = c.x[:, :, :].rearrange("p t d -> p (t d)")
        xd_flat = m.xd[:, :, :].rearrange("p t n -> p (t n)")
        bt_flat = m.btok[:, :, :].rearrange("p t n -> p (t n)")

        def real(n, it):
            return it is not None or 0 <= n < NT

        def at(sem, n, j=1, it=None):
            k = per[sem]
            return count(sem, k * n + j, None if it is None else (it, 2 * k))

        def tile(n, width, it):
            return slice(n * width, (n + 1) * width) if it is None else bass.ds(it * (2 * width) + n * width, width)

        def spans(eng, program):
            for n in (-1, 0, 1):
                program(n, None)
            with eng.Fori(0, NT // 2 - 2, 1) as it:
                for n in (2, 3):
                    program(n, it)
            for n in range(NT - 2, NT + 2):
                program(n, None)

        def back(n, g, k):
            return (n, g - k) if g >= k else (n - 1, g - k + NG)

        with nc.Block() as block:
            @block.tensor
            def _(pe):
                def step(n, it):
                    for g in range(NG):
                        if real(n, it):
                            pe.wait_ge(rb_done, at(rb_done, n, g + 1, it))
                            n2, g2 = back(n, g, 2)
                            if real(n2, it):
                                pe.wait_ge(l_done, at(l_done, n2, g2 + 1, it))
                            for part in range(2):
                                ins = pe.matmul(banks[:, g % 2, :], later[:, :],
                                                rbuf[g % 2][:, part, :, :].rearrange("p h l -> p (h l)"),
                                                start=part == 0, stop=part == 1)
                            ins.then_inc(seg_done, 1)
                        if g == 1 and real(n + 1, it):
                            if real(n - 2, it):
                                pe.wait_ge(x_done, at(x_done, n - 2, 1, it))
                            elif real(n, it):
                                pe.wait_ge(gm_done, at(gm_done, n, 1, it))
                            pe.wait_ge(stage_done, at(stage_done, n + 1, 1, it))
                            bc = bcs[(n + 1) % 2]
                            pe.matmul(shared[:, 0:P], bc[:, 0, :], bc[:, 1, :], start=True, stop=True).then_inc(g_done, 1)
                        if g in (4, 7) and real(n, it):
                            j = int(g == 7)
                            if g == 4:
                                pe.wait_ge(stage_done, at(stage_done, n, 1, it))
                                if real(n + 1, it):
                                    pe.wait_ge(gm_done, at(gm_done, n + 1, 1, it))
                                pe.wait_ge(xdr_done, at(xdr_done, n, 1, it))
                                if real(n - 1, it):
                                    pe.wait_ge(y_done, at(y_done, n - 1, 1, it))
                                    pe.wait_ge(upd_done, at(upd_done, n - 1, 2, it))
                                else:
                                    pe.wait_ge(init_done, count(init_done, 1))
                            else:
                                pe.wait_ge(upd_done, at(upd_done, n, 1, it))
                            pe.matmul(banks[0:CH, 4 + j, :], bcs[n % 2][:, 1, j * CH:(j + 1) * CH],
                                      state[j][:, :], start=True, stop=True).then_inc(off_done, 1)
                            pe.matmul(banks[:, 6, :], bts[n % 2][j * CH:(j + 1) * CH, :],
                                      xdr[n % 2][j * CH:(j + 1) * CH, :], start=True, stop=True).then_inc(st_done, 1)
                        if g == 4 and real(n - 1, it):
                            if it is None:
                                pe.wait_ge(y_done, at(y_done, n - 1, 1, it))
                                if not real(n + 1, it):
                                    pe.wait_ge(x_done, at(x_done, n - 2, 1, it))
                            for ch in range(2):
                                for j in range(NZ):
                                    ins = pe.transpose(shared[:, j * P + ch * CH:j * P + (ch + 1) * CH],
                                                       ysb[:, ch, j * P:(j + 1) * P], c.ident[0:CH, 0:CH])
                            ins.then_inc(t_done, 1)
                        if g == 7 and real(n - 1, it):
                            pe.wait_ge(sq_done, at(sq_done, n - 1, 1, it))
                            pe.wait_ge(gz_done, at(gz_done, n - 1, 1, it))
                            for j in range(NZ):
                                pe.matmul(shared[:, D:D + 1], sq[:, j, :], m.ones, start=j == 0, stop=j == NZ - 1)
                            for j in range(NZ):
                                ins = pe.matmul(shared[:, 0:D], gz[:, j, :], m.w_out[:, j, :],
                                                start=j == 0, stop=j == NZ - 1)
                            ins.then_inc(out_done, 1)
                        n2, g2 = back(n, g, 2)
                        if real(n2, it):
                            pe.wait_ge(m_done, at(m_done, n2, g2 + 1, it))
                            if g2 == 0:
                                pe.wait_ge(xdb_done, at(xdb_done, n2, 1, it))
                                if real(n2 - 1, it):
                                    pe.wait_ge(y_done, at(y_done, n2 - 1, 1, it))
                            for h in range(8):
                                hh = 8 * g2 + h
                                ins = pe.matmul(diag[:, hh * 16:(hh + 1) * 16], mbuf[g2 % 2][:, h, :],
                                                xdb[n2 % 2][:, hh, :, :].rearrange("p c q -> p (c q)"),
                                                start=True, stop=True)
                            ins.then_inc(yd_done, 1)
                spans(pe, step)

            @block.scalar
            def _(a):
                a.activation(later[:, :], m.later, ACT.Copy)
                a.activation(dA_hi[:, :], m.dA[:, :], ACT.Copy).then_inc(split_done, 1)

                def step(n, it):
                    for g in range(NG):
                        if g == 0 and real(n + 1, it):
                            k = n + 1
                            if real(n - 1, it):
                                a.wait_ge(st_done, at(st_done, n - 1, 2, it))
                            a.activation(bcs[k % 2][:, :, :], m.bcT[:, :, tile(k, P, it)], ACT.Copy)
                            a.activation(bts[k % 2][:, :], bt_flat[:, tile(k, P, it)], ACT.Copy).then_inc(stage_done, 1)
                        if g == 2 and real(n + 1, it):
                            k = n + 1
                            if real(n - 1, it):
                                a.wait_ge(yd_done, at(yd_done, n - 1, 8, it))
                            else:
                                a.wait_ge(init_done, count(init_done, 1))
                            for ch in range(2):
                                rows = slice(ch * CH, (ch + 1) * CH)
                                ins = a.activation(xdb[k % 2][rows, :, ch, :], xd_flat[rows, tile(k, INNER, it)]
                                                   .rearrange("p (h q) -> p h q", q=HP), ACT.Copy)
                            ins.then_inc(xdb_done, 1)
                        if real(n, it):
                            a.wait_ge(seg_done, at(seg_done, n, g + 1, it))
                            n2, g2 = back(n, g, 2)
                            if real(n2, it):
                                a.wait_ge(m_done, at(m_done, n2, g2 + 1, it))
                            a.activation(lbuf[g % 2][:, :, :].rearrange("p h l -> p (h l)"),
                                         banks[:, g % 2, :], ACT.Exp).then_inc(l_done, 1)
                        if g == 6 and real(n - 1, it):
                            a.wait_ge(gz_done, at(gz_done, n - 1, 1, it))
                            if real(n - 2, it):
                                a.wait_ge(out_done, at(out_done, n - 2, 1, it))
                            a.activation(sq[:, :, :], gz[:, :, :], ACT.Square).then_inc(sq_done, 1)
                spans(a, step)

            @block.gpsimd
            def _(q):
                q.memset(state[0][:, :], 0.0)
                for i in range(2):
                    q.memset(xdb[i][:, :, :, :], 0.0)
                q.memset(var[:, 3:4], -0.5).then_inc(init_done, 1)
                q.wait_ge(split_done, count(split_done, 1))
                q.tensor_tensor(dA_lo[:, :], m.dA[:, :], dA_hi[:, :].bitcast(F32), ALU.subtract).then_inc(pool, 1)
                q.wait_ge(pool, own(pool))

                def step(n, it):
                    for g in range(NG):
                        k, gk = (n, g + 2) if g + 2 < NG else (n + 1, g + 2 - NG)
                        if real(k, it):
                            if real(n, it):
                                q.wait_ge(seg_done, at(seg_done, n, g + 1, it))
                            heads = (slice(NH * k + 8 * gk, NH * k + 8 * gk + 8) if it is None
                                     else bass.ds(it * (2 * NH) + (NH * k + 8 * gk), 8))
                            for part, d in enumerate((dA_hi[:, heads].bitcast(F32), dA_lo[:, heads])):
                                ins = q.tensor_tensor(rbuf[gk % 2][:, part, :, :], bx(d, CH), ax(m.within, 8), ALU.mult)
                            ins.then_inc(rb_done, 1)
                        if g == 0 and real(n - 2, it):
                            q.wait_ge(var_done, at(var_done, n - 2, 1, it))
                            q.wait_ge(init_done, count(init_done, 1))
                            q.tensor_tensor(var[:, 1:2], var[:, 0:1], var[:, 3:4], ALU.pow).then_inc(pow_done, 1)
                spans(q, step)

            @block.vector
            def _(v):
                def step(n, it):
                    for g in range(NG):
                        if g == 1 and real(n - 2, it):
                            k = n - 2
                            v.wait_ge(pow_done, at(pow_done, k, 1, it))
                            xs = x_flat[:, tile(k, D, it)]
                            v.scalar_tensor_tensor(out=xs, in0=shared[:, 0:D], scalar=var[:, 1:2], in1=xs,
                                                   op0=ALU.mult, op1=ALU.add).then_inc(x_done, 1)
                        n1, g1 = back(n, g, 1)
                        if real(n1, it):
                            v.wait_ge(l_done, at(l_done, n1, g1 + 1, it))
                            if g1 == 0:
                                v.wait_ge(gm_done, at(gm_done, n1, 1, it))
                            n3, g3 = back(n, g, 3)
                            if real(n3, it):
                                v.wait_ge(yd_done, at(yd_done, n3, g3 + 1, it))
                            v.tensor_tensor(mbuf[g1 % 2][:, :, :], lbuf[g1 % 2][:, :, :],
                                            ax(gm[n1 % 2][:, :], 8), ALU.mult).then_inc(m_done, 1)
                        if g == 0 and real(n - 2, it):
                            k = n - 2
                            v.wait_ge(out_done, at(out_done, k, 1, it))
                            v.tensor_scalar(var[:, 0:1], shared[:, D:D + 1], 1.0 / INNER, 1e-6,
                                            ALU.mult, ALU.add).then_inc(var_done, 1)
                        if g == 0 and real(n + 1, it):
                            k = n + 1
                            if real(n - 1, it):
                                v.wait_ge(st_done, at(st_done, n - 1, 2, it))
                            v.tensor_tensor(
                   xdr[k % 2][:, :].rearrange("p (h q) -> p h q", q=HP),
                   xd_flat[:, tile(k, INNER, it)].rearrange("p (h q) -> p h q", q=HP),
                   bx(m.rev[:, tile(k, NH, it)], HP), ALU.mult).then_inc(xdr_done, 1)
                        if g == 2 and real(n + 1, it):
                            k = n + 1
                            v.wait_ge(g_done, at(g_done, k, 1, it))
                            if real(n - 1, it):
                                v.wait_ge(m_done, at(m_done, n - 1, 8, it))
                            for ch in range(2):
                                rows = slice(ch * CH, (ch + 1) * CH)
                                ins = v.tensor_tensor(gm[k % 2][rows, :], shared[rows, rows], m.within[rows, :],
                                                      ALU.mult)
                            ins.then_inc(gm_done, 1)
                        if g == 1 and real(n - 1, it):
                            k = n - 1
                            v.wait_ge(off_done, at(off_done, k, 2, it))
                            if real(n - 2, it):
                                v.wait_ge(t_done, at(t_done, n - 2, 1, it))
                            for ch in range(2):
                                ins = v.tensor_tensor(ysb[:, ch, :].rearrange("p (h q) -> p h q", q=HP),
                                                      banks[0:CH, 4 + ch, :].rearrange("p (h q) -> p h q", q=HP),
                                                      bx(m.head[:, ch, tile(k, NH, it)], HP), ALU.mult)
                            ins.then_inc(y1_done, 1)
                        if g == 2 and real(n - 1, it):
                            k = n - 1
                            v.wait_ge(y1_done, at(y1_done, k, 1, it))
                            v.wait_ge(yd_done, at(yd_done, k, 8, it))
                            for ch in range(2):
                                y = ysb[:, ch, :].rearrange("p (h q) -> p h q", q=HP)
                                ins = v.tensor_tensor(y, y, diag.rearrange("p (h c q) -> p h c q", c=2, q=HP)[:, :, ch, :],
                                                      ALU.add)
                            ins.then_inc(y_done, 1)
                        if g in (5, 7) and real(n, it):
                            j = int(g == 7)
                            if n or j or it is not None:
                                v.wait_ge(upd_done, at(upd_done, n if j else n - 1, 1 if j else 2, it))
                            else:
                                v.wait_ge(init_done, count(init_done, 1))
                            v.tensor_tensor(tmp[:, :].rearrange("p (h q) -> p h q", q=HP),
                                            state[j][:, :].rearrange("p (h q) -> p h q", q=HP),
                                            bx(m.tot[:, j, tile(n, NH, it)], HP), ALU.mult).then_inc(tmp_done, 1)
                            v.wait_ge(tmp_done, at(tmp_done, n, j + 1, it))
                            v.wait_ge(st_done, at(st_done, n, j + 1, it))
                            v.tensor_tensor(state[1 - j][:, :], tmp[:, :], banks[:, 6, :], ALU.add).then_inc(upd_done, 1)
                        if g == 5 and real(n - 1, it):
                            k = n - 1
                            v.wait_ge(t_done, at(t_done, k, 1, it))
                            if real(n - 2, it):
                                v.wait_ge(out_done, at(out_done, n - 2, 1, it))
                            for j in range(NZ):
                                ins = v.scalar_tensor_tensor(out=yT[:, j, :], in0=m.xT[:, j, tile(k, P, it)],
                                                             scalar=m.d_col[:, j:j + 1],
                                                             in1=shared[:, j * P:(j + 1) * P],
                                                             op0=ALU.mult, op1=ALU.add)
                            ins.then_inc(yt_done, 1)
                        if g == 6 and real(n - 1, it):
                            k = n - 1
                            v.wait_ge(yt_done, at(yt_done, k, 1, it))
                            v.tensor_tensor(gz[:, :, :], yT[:, :, :], m.zT[:, :, tile(k, P, it)], ALU.mult).then_inc(gz_done, 1)
                spans(v, step)
        counts = {s: k * NT for s, k in per.items()}
        counts.update({init_done: 1, split_done: 1})
        c.done(counts)



class WeightRing:

    def __init__(self, c):
        shapes = ([P, DK, GW], [P, G, D])
        names = ("wqkv", "wo")
        self.raw = [c.sb(f"{name}_raw", shape) for name, shape in zip(names, shapes)]
        self.parts = [[[c.sb(f"{name}_{part}{i}", shape, F32R) for part in ("hi", "lo")] for i in range(2)]
                      for name, shape in zip(names, shapes)]
        self.rope = c.sb("rope", [P, 2, NT, HD])
        self.rope_loaded = c.sem("rope_loaded")
        self.loaded, self.hi_done, self.lo_done = (
            [c.sem(f"{name}_{what}") for name in names] for what in ("loaded", "hi", "lo"))


class AttentionWeights:

    def __init__(self, c, ring, name, dram):
        self.c, self.raw, self.parts = c, ring.raw, ring.parts
        self.loaded, self.hi_done, self.lo_done = ring.loaded, ring.hi_done, ring.lo_done
        self.rope, self.rope_loaded = ring.rope, ring.rope_loaded
        self.rope_dram = dram[name + "_rope"]
        self.dram = [dram[f"{name}_{part}"].rearrange("g p n -> (g p) n") for part in ("wqkv", "wo")]

    def at(self, sem, n, k, it):
        return self.c.count(sem, k * (n + 1), None if it is None else (it, 2 * k))

    def load(self, sp, part, rows):
        sp.dma_start(self.raw[part][:, :, :].rearrange("p k n -> p (k n)"), self.dram[part][rows, :])\
            .then_inc(self.loaded[part], 16)

    def load_first(self, sp):
        sp.dma_start(self.rope[:, :, :, :], self.rope_dram).then_inc(self.rope_loaded, 16)
        for part in range(2):
            self.load(sp, part, slice(0, P))


def add_residual(c):
    with c.nc.Block() as block:
        @block.vector
        def _(v):
            v.tensor_tensor(c.x[:, :, :], c.x[:, :, :], c.u[:, :, :], ALU.add)


def hybrid_program(nc, d, out):
    with ExitStack() as ctx:
        c = Core(nc, ctx, d)
        wg = c.sb("wg", [P, DK, NE])
        gates = c.sb("gates", [P, NE, NT])
        loads = ctx.enter_context(nc.semaphore("loads"))
        stored = ctx.enter_context(nc.semaphore("stored"))

        with ExitStack() as mctx:
            m = MambaMemory(c, mctx)
            with nc.Block() as block:
                @block.sync
                def _(sp):
                    sp.dma_start(c.x[:, :, :], d["x"].rearrange("(t p) d -> p t d", p=P)).then_inc(loads, 16)
                    sp.dma_start(c.ident[:, :], d["ident"]).then_inc(loads, 16)
                    sp.dma_start(c.consts[:, :], d["consts"]).then_inc(loads, 16)
                    sp.dma_start(m.w_in[:, :, :], d["w_in"].rearrange("(k p) n -> p k n", p=P)).then_inc(loads, 16)
                    sp.dma_start(m.cols[:, :], d["cols"]).then_inc(loads, 16)
                    sp.dma_start(m.rows[:, :], d["rows"].partition_broadcast(P)).then_inc(loads, 16)
                    sp.dma_start(m.scan[:, :], d["scan"]).then_inc(loads, 16)
                    sp.dma_start(m.w_out[:, :, :], d["w_out"].rearrange("(k p) n -> p k n", p=P)).then_inc(loads, 16)
                    sp.dma_start(wg[:, :, :], d["wg"].rearrange("(k p) n -> p k n", p=P)).then_inc(loads, 16)
                    sp.dma_start(c.ln_cols[:, :, :], d["ln_cols"]).then_inc(loads, 16)

                @block.vector
                def _(v):
                    v.wait_ge(loads, 160)
                    v.tensor_copy(c.ident16[:, :], c.ident[:, :])
                    v.tensor_copy(c.causal16[:, :], c.consts[:, P:2 * P])
            normalise(c, c.x, True, None, None, m.hT, c.u)
            mamba_front(c, m)
            mamba_scan(c, m)

        ring = WeightRing(c)
        ffn = AttentionWeights(c, ring, "ffn", d)
        attn = AttentionWeights(c, ring, "attn", d)
        h_hi, h_lo = (c.sb(f"h_{part}", [P, DK, L], F32R) for part in ("hi", "lo"))

        def attend(weights, cols, eps, acc):
            with ExitStack() as actx:
                hT = c.sb(f"hT{c.phase}", [P, DK, L], F32, actx)
                normalise(c, c.x, True, eps, cols, hT, c.u, (h_hi, h_lo), weights)
            attention(c, (h_hi, h_lo), weights, acc)

        def feed_forward():
            attend(ffn, c.ln_cols[:, 0, :], 1e-5, c.u)
            with ExitStack() as fctx:
                hT = c.sb(f"hT{c.phase}", [P, DK, L], F32, fctx)
                w = ExpertWeights(c, fctx, d["experts"])
                normalise(c, c.u, False, 1e-5, c.ln_cols[:, 1, :], hT, None, (h_hi, h_lo), loads=w)
                router(c, hT, wg, gates)
                experts(c, h_hi, h_lo, gates, w, c.u)

        feed_forward()
        add_residual(c)
        attend(attn, None, None, c.x)
        feed_forward()
        add_residual(c)
        with nc.Block() as block:
            @block.sync
            def _(sp):
                sp.dma_start(out.rearrange("(t p) d -> p t d", p=P), c.x[:, :, :]).then_inc(stored, 16)
                sp.wait_ge(stored, 16)



def _rotary(base_exponents):
    ang = np.arange(L, dtype=np.float32)[:, None] * base_exponents[None, :]
    cos, sin = np.cos(ang), np.sin(ang)
    table = np.stack([np.concatenate([cos, cos], -1), np.concatenate([-sin, sin], -1)])
    return np.ascontiguousarray(table.reshape(2, NT, P, HD).transpose(2, 0, 1, 3))


def _grouped(wq, wk, wv):
    w = np.concatenate([wq.reshape(D, HKV, G * HD), wk.reshape(D, HKV, HD), wv.reshape(D, HKV, HD)], -1)
    return np.ascontiguousarray(w.reshape(DK, P, HKV, GW).transpose(2, 1, 0, 3).reshape(HKV, P, DK * GW))


def _twice(wo):
    w = wo.reshape(HKV, G, HD, D).transpose(0, 2, 1, 3).reshape(HKV, HD, G * D)
    return np.ascontiguousarray(np.concatenate([w, w], 1))


def _scan_constants():
    t = np.arange(P)
    chunk, place = t // CH, t % CH
    later = (t[:, None] > t[None, :]) & (chunk[:, None] == chunk[None, :])
    upto = np.stack([(chunk[:, None] == k) & (place[:, None] <= np.arange(CH)[None, :]) for k in range(2)], 1)
    whole = np.stack([np.repeat((chunk == k)[:, None], P, 1) for k in range(2)], 1)
    within = place[:, None] <= np.arange(CH)[None, :]
    parts = [later, upto.reshape(P, -1), whole.reshape(P, -1), within, np.zeros((P, CH)), np.ones((P, CH))]
    return np.concatenate([np.asarray(p, np.float32) for p in parts], 1)


def kernel(**inputs):
    import concourse.bacc as bacc
    from concourse.bass_utils import run_bass_kernel_spmd

    a = {k: np.asarray(v) for k, v in inputs.items()}
    A, B, F = "L0_attn_a_", "L0_attn_b_", "L0_ffn_"
    cols = lambda v: v.reshape(-1, P).T
    b_in = a[A + "b_in"]
    split_b = INNER + CONVD
    taps = a[A + "conv_w"].reshape(TAPS, NX, P).transpose(2, 1, 0).reshape(P, NX * TAPS)
    halves = np.concatenate([np.arange(0, HD, 2), np.arange(1, HD, 2)])
    turned = lambda w: w.T.reshape(D, -1, HD)[:, :, halves].reshape(D, -1)
    place = np.arange(P)
    e32 = np.arange(HD // 2, dtype=np.float32)
    arrays = {
        "x": a[A + "x"].reshape(L, D),
        "ident": np.eye(P, dtype=np.float32),
        "consts": np.concatenate([np.tile(np.arange(P, dtype=np.float32), (P, 1)),
                                  np.where(place[:, None] >= place[None, :], 0.0, NEG).astype(np.float32)], 1),
        "w_in": a[A + "W_in"],
        "w_out": a[A + "W_out"],
        "cols": np.concatenate([cols(b_in[:split_b]), taps, cols(a[A + "conv_b"]),
                                cols(np.repeat(a[A + "D_param"], HP)), cols(a[A + "norm_w"])], 1),
        "rows": np.concatenate([b_in[split_b:], a[A + "dt_bias"], a[A + "A_log"], a[A + "b_out"]]),
        "scan": _scan_constants(),
        "wg": a[F + "wg"],
        "ln_cols": np.stack([cols(a[F + "ln_w"]), cols(a[F + "ff_ln_w"])], 1),
        "ffn_wqkv": _grouped(a[F + "wq"], a[F + "wk"], a[F + "wv"]),
        "ffn_wo": _twice(a[F + "wo"]),
        "ffn_rope": _rotary(np.float32(1.0) / np.float32(150000.0) ** (e32 / np.float32(HD // 2))),
        "attn_wqkv": _grouped(turned(a[B + "Wq"]), turned(a[B + "Wk"]), a[B + "Wv"].T),
        "attn_wo": _twice(a[B + "Wo"].T),
        "attn_rope": _rotary(np.float32(1.0) / np.float32(10000.0) ** (e32 * np.float32(2) / np.float32(HD))),
        "experts": np.stack([a[F + "w1"], a[F + "w3"], a[F + "w2"]], 1).reshape(NE, 3, DK, P, HH)
                     .transpose(0, 3, 1, 2, 4).reshape(NE, P, 3 * DK * HH),
    }
    nc = bacc.Bacc("TRN2", target_bir_lowering=False, num_devices=1)
    d, feed = {}, {}
    for name, v in arrays.items():
        feed["in_" + name] = np.ascontiguousarray(v)
        d[name] = nc.dram_tensor("in_" + name, v.shape, F32, kind="ExternalInput").ap()
    out = nc.dram_tensor("out_dram", (L, D), F32, kind="ExternalOutput").ap()
    hybrid_program(nc, d, out)
    r = run_bass_kernel_spmd(nc, [feed], core_ids=[0])
    return r.results[0]["out_dram"].reshape(1, L, D)
```
